# Optimizing a Trainium2 kernel written in Bass

```python
import numpy as np
import jax
import jax.numpy as jnp

def _softmax(x, axis=-1):
    return jax.nn.softmax(x, axis=axis)

def _gelu(x):
    return jax.nn.gelu(x, approximate=True)

def _silu(x):
    return jax.nn.silu(x)

def _sigmoid(x):
    return jax.nn.sigmoid(x)

def _layernorm(x, axis=-1, eps=1e-05):
    m = jnp.mean(x, axis=axis, keepdims=True)
    v = jnp.var(x, axis=axis, keepdims=True)
    return (x - m) / jnp.sqrt(v + eps)

def _scatter_add(tgt, idx, src, axis=0):
    return tgt.at[idx].add(src)

def _segment_sum(src, seg, n):
    return jax.ops.segment_sum(src, seg, n)
kernel_name = 'mk_xattn_ffn_d1_seqx_r8_c1fb85'

def setup_inputs(seed: int=0):
    np.random.seed(seed)
    _w = jnp.asarray

    def _rec_inputs():
        import jax
        import jax.numpy as jnp
        _rk = jax.random.key(seed)
        x = 7.22e-05 + 1 * jax.random.normal(jax.random.fold_in(_rk, 1), (32, 64, 128), jnp.float32)
        _lenS = 64 - jax.random.randint(jax.random.fold_in(_rk, 7), (32,), 0, max(1, 64 // 4) + 1, jnp.int32)
        _lenS2 = 64 - jax.random.randint(jax.random.fold_in(_rk, 8), (32,), 0, max(1, 64 // 4) + 1, jnp.int32)
        _ctx_768P = jax.random.normal(jax.random.fold_in(_rk, 11), (32, 16, 96), jnp.float32)
        _ctx_768c = jax.random.dirichlet(jax.random.fold_in(_rk, 511), 0.3 * jnp.ones((16,), jnp.float32), (32, 64))
        _ctx_768t = jnp.einsum('bsk,bkd->bsd', _ctx_768c, _ctx_768P)
        _ctx_768t = _ctx_768t * jax.lax.rsqrt(jnp.mean(jnp.square(_ctx_768t)) + 1e-12) * 0.953939
        ctx_768 = -0.000191848 + 0.999787 * (_ctx_768t + 0.3 * jax.random.normal(jax.random.fold_in(_rk, 611), (32, 64, 96), jnp.float32))
        return (x, ctx_768)
    x, ctx_768 = _rec_inputs()

    def _L0_xattn_setup():
        import jax, jax.numpy as jnp
        import numpy as np
        Q_DIM = 128
        KV_DIM = 96
        HEADS = 16
        DK = Q_DIM // HEADS
        key = jax.random.key(seed)
        ks = jax.random.split(key, 6)
        B, T_q, T_kv = (4, 256, 256)
        s_q = 1.0 / np.sqrt(Q_DIM)
        s_kv = 1.0 / np.sqrt(KV_DIM)
        return {'q_tokens': jax.random.normal(ks[0], (B, T_q, Q_DIM), jnp.float32), 'kv_tokens': jax.random.normal(ks[1], (B, T_kv, KV_DIM), jnp.float32), 'Wq': jax.random.normal(ks[2], (Q_DIM, Q_DIM), jnp.float32) * s_q, 'Wk': jax.random.normal(ks[3], (Q_DIM, KV_DIM), jnp.float32) * s_kv, 'Wv': jax.random.normal(ks[4], (Q_DIM, KV_DIM), jnp.float32) * s_kv, 'Wo': jax.random.normal(ks[5], (Q_DIM, Q_DIM), jnp.float32) * s_q}
    _L0_xattn_all = _L0_xattn_setup()
    _L0_xattn_in = {k: v for k, v in _L0_xattn_all.items() if k in ('Wq', 'Wk', 'Wv', 'Wo')}
    del _L0_xattn_all

    def _L0_ffn_setup():
        import jax, jax.numpy as jnp
        import numpy as np
        B, S, D, E, F = (2, 256, 128, 8, 512)
        key = jax.random.key(seed)
        ks = jax.random.split(key, 4)
        return {'hidden_states': jax.random.normal(ks[0], (B, S, D), dtype=jnp.float32), 'Wr': jax.random.normal(ks[1], (D, E), dtype=jnp.float32) * (1.0 / np.sqrt(D)), 'W1': jax.random.normal(ks[2], (E, D, F), dtype=jnp.float32) * (1.0 / np.sqrt(D)), 'b1': jnp.zeros((E, F), dtype=jnp.float32), 'W2': jax.random.normal(ks[3], (E, F, D), dtype=jnp.float32) * (1.0 / np.sqrt(F)), 'b2': jnp.zeros((E, D), dtype=jnp.float32)}
    _L0_ffn_all = _L0_ffn_setup()
    _L0_ffn_in = {k: v for k, v in _L0_ffn_all.items() if k in ('Wr', 'W1', 'b1', 'W2', 'b2')}
    del _L0_ffn_all
    return {'x': x, 'ctx_768': ctx_768, 'L0_xattn_Wq': _L0_xattn_in['Wq'], 'L0_xattn_Wk': _L0_xattn_in['Wk'], 'L0_xattn_Wv': _L0_xattn_in['Wv'], 'L0_xattn_Wo': _L0_xattn_in['Wo'], 'L0_ffn_Wr': _L0_ffn_in['Wr'], 'L0_ffn_W1': _L0_ffn_in['W1'], 'L0_ffn_b1': _L0_ffn_in['b1'], 'L0_ffn_W2': _L0_ffn_in['W2'], 'L0_ffn_b2': _L0_ffn_in['b2']}

def reference(x, ctx_768, L0_xattn_Wq, L0_xattn_Wk, L0_xattn_Wv, L0_xattn_Wo, L0_ffn_Wr, L0_ffn_W1, L0_ffn_b1, L0_ffn_W2, L0_ffn_b2):
    import jax
    import jax.numpy as jnp

    def _L0_xattn_ref(q_tokens, kv_tokens, Wq, Wk, Wv, Wo):
        import jax, jax.numpy as jnp
        import numpy as np
        Q_DIM = 128
        KV_DIM = 96
        HEADS = 16
        DK = Q_DIM // HEADS
        B, T_q, _ = q_tokens.shape
        T_kv = kv_tokens.shape[1]
        q = q_tokens @ Wq.T
        k = kv_tokens @ Wk.T
        v = kv_tokens @ Wv.T
        q = q.reshape(B, T_q, HEADS, DK).transpose(0, 2, 1, 3)
        k = k.reshape(B, T_kv, HEADS, DK).transpose(0, 2, 1, 3)
        v = v.reshape(B, T_kv, HEADS, DK).transpose(0, 2, 1, 3)
        scale = 1.0 / jnp.sqrt(jnp.asarray(DK, q.dtype))
        attn = jnp.einsum('bhqd,bhkd->bhqk', q, k) * scale
        attn = jax.nn.softmax(attn, axis=-1)
        out = jnp.einsum('bhqk,bhkd->bhqd', attn, v)
        out = out.transpose(0, 2, 1, 3).reshape(B, T_q, Q_DIM)
        return out @ Wo.T

    def _L0_ffn_ref(hidden_states, Wr, W1, b1, W2, b2):
        import jax, jax.numpy as jnp
        import numpy as np
        B, S, D, E, F = (2, 256, 128, 8, 512)
        b, s, d = hidden_states.shape
        e = Wr.shape[1]
        x = hidden_states.reshape(b * s, d)
        router_logits = x @ Wr
        router_probs = jax.nn.softmax(router_logits, axis=-1)
        expert_idx = jnp.argmax(router_probs, axis=-1)
        p_max = jnp.max(router_probs, axis=-1, keepdims=True)

        def expert_mlp(w1, bb1, w2, bb2):
            h = jax.nn.gelu(x @ w1 + bb1, approximate=False)
            return h @ w2 + bb2
        outs = jax.vmap(expert_mlp)(W1, b1, W2, b2)
        onehot = jax.nn.one_hot(expert_idx, e, dtype=x.dtype)
        next_states = jnp.einsum('te,etd->td', onehot, outs)
        out = p_max * next_states
        return out.reshape(b, s, d)
    x = x + _L0_xattn_ref(_layernorm(x, axis=-1), ctx_768, L0_xattn_Wq, L0_xattn_Wk, L0_xattn_Wv, L0_xattn_Wo)
    x = x + _L0_ffn_ref(_layernorm(x, axis=-1), L0_ffn_Wr, L0_ffn_W1, L0_ffn_b1, L0_ffn_W2, L0_ffn_b2)
    return x

_drawn_inputs = setup_inputs


def setup_inputs(seed=0):
    import zlib

    import numpy as np

    out = dict(_drawn_inputs(seed))
    spreads = {'L0_ffn_b1': (0.0, 0.355), 'L0_ffn_b2': (0.0, 0.1)}
    factors = {}
    for name, (base, spread) in spreads.items():
        noise = np.random.default_rng([zlib.crc32(name.encode()), seed]).standard_normal(out[name].shape)
        drawn = base * np.exp(spread * noise) if base else spread * noise
        out[name] = jnp.asarray(drawn.astype(out[name].dtype))
    for name, factor in factors.items():
        out[name] = (out[name] * factor).astype(out[name].dtype)
    return out
```

```python
import numpy as np
from contextlib import ExitStack

import concourse.bass as bass
from concourse import mybir
from concourse.alu_op_type import AluOpType as ALU

B, S, D = 32, 64, 128
KV = 96
H = 16
DK = D // H
E, F = 8, 512
P = 128
TOK = B * S
TILES = TOK // P
GROUPS = 4
GB = B // GROUPS
GT = TILES // GROUPS
GC = TOK // GROUPS
HP = H // 2
C = HP // 2
VC = 2 * DK + 2
FC = F // P
RW = D + 4
MEAN, VAR, RSTD, TOP = D, D + 1, D + 2, D + 3
SLOTS = TILES
CODES = E * SLOTS
JOBS = TILES + E - 1
JC = JOBS + 1
EARLY = TILES - 4
EPS = 1e-5
NOWHERE = 4095


def build(nc, a):
    f32, f16, i32, u32 = mybir.dt.float32, mybir.dt.float16, mybir.dt.int32, mybir.dt.uint32
    ACT, AX = mybir.ActivationFunctionType, mybir.AxisListType
    ds = bass.ds
    ctx = ExitStack()
    with ctx:
        def sb(name, shape, dt=f32):
            return ctx.enter_context(nc.sbuf_tensor(name, shape, dt))

        def sem(name):
            return ctx.enter_context(nc.semaphore(name))

        ident = sb("ident", [P, P])
        parity = sb("parity", [P, 2])
        wq, wo = sb("wq", [D, D]), sb("wo", [D, D])
        wk, wv = sb("wk", [KV, D]), sb("wv", [KV, D])
        wr = sb("wr", [D, E])
        ctx_t = sb("ctx_t", [KV, TOK])
        rows = sb("rows", [P, TILES, RW])
        stats = sb("stats", [P, TILES, 6])
        moments = sb("moments", [P, TILES, 2])
        rstd1 = sb("rstd1", [P, TILES])
        zero = sb("zero", [P, 1])
        neg_half, eps = sb("neg_half", [P, TILES]), sb("eps", [P, TILES])
        q_t = sb("q_t", [D, TOK])
        k_t = sb("k_t", [D, TOK])
        k_diag = sb("k_diag", [D, HP, TOK])
        v_diag = sb("v_diag", [P, B, C, 2, VC])
        q_par = sb("q_par", [D, 2, 2, S])
        s_max = sb("s_max", [P, 2, HP])
        v_now = sb("v_now", [P, C, 2, VC])
        work = sb("work", [P, TILES * D])
        xn = work[:, :].rearrange("p (t d) -> p t d", t=TILES)
        s_sub = work[:, 0:2 * HP * S].rearrange("p (k n) -> p k n", k=2)
        p_t = work[:, 2 * HP * S:4 * HP * S].rearrange("p (k n) -> p k n", k=2)
        den = sb("den", [P, 2 * C, 2])
        o_sb = sb("o_sb", [P, D])
        o_t = sb("o_t", [D, P])
        stats2 = sb("stats2", [P, 6])
        vare = sb("vare", [P, 1])
        row = sb("row", [P, TOP])
        xc = sb("xc", [P, D])
        xn2 = sb("xn2", [P, D])
        xn2_t = sb("xn2_t", [D, P])
        top = sb("top", [P, 1])
        logit = sb("logit", [P, TILES, E])
        gexp = sb("gexp", [P, E])
        gsum = sb("gsum", [P, TILES])
        tri = sb("tri", [P, P], f16)
        ones = sb("ones", [P, P], f16)
        first = sb("first", [P, E])
        token1 = sb("token1", [P, TILES])
        count_up = sb("count_up", [P, P])
        position = sb("position", [P, P], f16)
        code_row = sb("code_row", [P, CODES], f16)
        partition = sb("partition", [P, 1])
        cand = sb("cand", [P, TILES, E])
        best = sb("best", [P, TILES])
        onehot = sb("onehot", [P, TILES, E], f16)
        ranked = sb("ranked", [P, TILES, E])
        rank = sb("rank", [P, TILES])
        rank_i = sb("rank_i", [P, TILES], i32)
        slot_i = sb("slot_i", [P, TILES], i32)
        pos = sb("pos", [P, TILES])
        code = sb("code", [P, TILES])
        where_pos = k_diag[:, 0, 0:TILES * P // 2].bitcast(f16).rearrange("p (t n) -> p t n", n=P)
        where_code = k_diag[:, 0, TILES * P // 2:TILES * P].bitcast(f16).rearrange("p (t n) -> p t n", n=CODES)
        cnt_i = sb("cnt_i", [P, 2, E], i32)
        ends = sb("ends", [P, E])
        past = sb("past", [P, JC, E])
        past_n = sb("past_n", [P, JC, E])
        job = sb("job", [P, 4, JC])
        job_i = sb("job_i", [P, JC], i32)
        pick = sb("pick", [CODES, JC])
        table = sb("table", [CODES, P])
        slots = sb("slots", [P, JC])
        empty = sb("empty", [P, JC])
        from_row = sb("from_row", [P, JC], i32)
        to_row = sb("to_row", [P, JC], i32)
        w1 = sb("w1", [D, E * F])
        w2 = sb("w2", [P, E * FC * D])
        b1 = sb("b1", [P, E * F])
        b2 = sb("b2", [P, E * D])
        NG, NR, NI = 6, 3, 3
        gathered = sb("gathered", [P, NG, RW])
        from_now = sb("from_now", [P, 2, NI], i32)
        to_now = sb("to_now", [P, 2, NI], i32)
        xf = sb("xf", [P, 2, D])
        xf_t = sb("xf_t", [D, 2, P])
        hid = k_diag[:, 1, 0:2 * F].rearrange("p (k n) -> p k n", k=2)
        hid_t = k_diag[:, 2, 0:2 * F].rearrange("p (k n) -> p k n", k=2)
        yb = sb("yb", [P, 2, D])
        res = sb("res", [P, NR, D])

        bank = [ctx.enter_context(nc.psum_tensor(f"bank{i}", [P, 512], f32)) for i in range(8)]
        x_mid = nc.dram_tensor("x_mid", [TOK, RW], f32, kind="Internal").ap()

        wk_in, w_in, ctx_in, const_in, ffn_in = sem("wk_in"), sem("w_in"), sem("ctx_in"), sem("const_in"), sem("ffn_in")
        x_in = [sem(f"x_in{g}") for g in range(GROUPS)]
        zero_set, filled = sem("zero_set"), sem("filled")
        zeroed = [sem(f"zeroed{g}") for g in range(GROUPS)]
        v_fixed = sem("v_fixed")
        stats_done, moments_done, rstd1_in, rstd1_done, xn_done = (
            sem("stats_done"), sem("moments_done"), sem("rstd1_in"), sem("rstd1_done"), sem("xn_done"))
        k_done, v_done, xt_done, q_done = sem("k_done"), sem("v_done"), sem("xt_done"), sem("q_done")
        k_out, v_out0, v_out1, xt_out, q_out = (
            sem("k_out"), sem("v_out0"), sem("v_out1"), sem("xt_out"), sem("q_out"))
        k_diag_in = sem("k_diag_in")
        v_now_done = sem("v_now_done")
        q_par_done, s_done, max_done, sub_done = sem("q_par_done"), sem("s_done"), sem("max_done"), sem("sub_done")
        st_done, exp_done, pv_done = sem("st_done"), sem("exp_done"), sem("pv_done")
        den_done, o_done, ot_done, ot_out, proj_done = (
            sem("den_done"), sem("o_done"), sem("ot_done"), sem("ot_out"), sem("proj_done"))
        xm_done, stats2_done, moments2_done, vare_done, rstd2_done, xn2_done = (
            sem("xm_done"), sem("stats2_done"), sem("moments2_done"), sem("vare_done"),
            sem("rstd2_done"), sem("xn2_done"))
        x2t_done, x2t_out, route_done, top_done, logit_done, gsum_done, row_done = (
            sem("x2t_done"), sem("x2t_out"), sem("route_done"), sem("top_done"),
            sem("logit_done"), sem("gsum_done"), sem("row_done"))
        row_kept, rows_out = sem("row_kept"), sem("rows_out")
        dve_met, pool_met = sem("dve_met"), sem("pool_met")
        step, step_done = sem("step"), sem("step_done")
        onehot_done, rank_done, places_done, table_done, table_out, jobs_done, slots_done, index_done = (
            sem("onehot_done"), sem("rank_done"), sem("places_done"), sem("table_done"), sem("table_out"),
            sem("jobs_done"), sem("slots_done"), sem("index_done"))
        from_done, to_done = sem("from_done"), sem("to_done")
        got = [sem(f"got{k}") for k in range(NG)]
        put = [sem(f"put{k}") for k in range(NR)]
        xf_done, xft_done, xft_out, h_done, hid_done, ht_done, gelu_done, y_done, yb_done, res_done = (
            sem("xf_done"), sem("xft_done"), sem("xft_out"), sem("h_done"), sem("hid_done"),
            sem("ht_done"), sem("gelu_done"), sem("y_done"), sem("yb_done"), sem("res_done"))

        def after(eng, s, n):
            if not (isinstance(n, int) and n <= 0):
                eng.wait_ge(s, n)

        def pipeline(eng, iteration, steady, loop_end, end):
            for i in range(steady):
                iteration(i)
            with eng.Fori(steady, loop_end) as i:
                iteration(i)
            for i in range(loop_end, end):
                iteration(i)

        def valid(i, n):
            return not isinstance(i, int) or 0 <= i < n

        def has_job(q, n):
            return not isinstance(q, int) or 0 <= n < JOBS

        FIRST = NR + 2
        AHEAD = 4

        def all_jobs(eng, do_job, at_start):
            at_start(0, 0)
            for n in range(FIRST):
                do_job(0, n)
            turns = (JOBS - FIRST - AHEAD) // NG
            with eng.Fori(0, turns) as q:
                at_start(q, FIRST)
                for n in range(FIRST, FIRST + NG):
                    do_job(q, n)
            at_start(0, FIRST + turns * NG)
            for n in range(FIRST + turns * NG, JOBS):
                do_job(0, n)

        def at(i, n):
            return isinstance(i, int) and i == n

        CONSTS = ((parity, "parity"), (tri, "tri"), (first, "first"), (token1, "token1"), (count_up, "count_up"),
                  (position, "position"), (code_row, "code_row"), (partition, "partition"))
        LAG_XM, LAG_ROUTE, LAG_ROW = 3, 4, 5
        PEEL, ATT_END = LAG_ROW, TILES + LAG_ROW

        def place_v(g, m, half, par):
            n = g * GB + m
            dst = v_diag[half * S:(half + 1) * S, n:n + GB - 1:2, :, par, half * DK:(half + 1) * DK]
            src = bank[3 + g % 2][m * S:(m + 1) * S, :].rearrange("p (t c m h d) -> p t c m h d", t=GT, m=2, h=2, d=DK)[:, :, :, half, par, :]
            return dst, src

        block = ctx.enter_context(nc.Block())

        @block.sync
        def _(sp):
            sp.dma_start(wk[:, :], a["wk"]).then_inc(wk_in, 16)
            sp.dma_start(ctx_t[:, :], a["ctx_t"]).then_inc(ctx_in, 16)
            xr = a["x"].rearrange("p (t d) -> p t d", d=D)
            for g in range(GROUPS):
                sp.dma_start(rows[:, g * GT:(g + 1) * GT, 0:D], xr[:, g * GT:(g + 1) * GT, :]).then_inc(x_in[g], 16)
            for dst, name in ((wv, "wv"), (wq, "wq"), (ident, "ident"), (wo, "wo"), (wr, "wr")):
                sp.dma_start(dst[:, :], a[name]).then_inc(w_in, 16)
            for dst, name in CONSTS:
                sp.dma_start(dst[:, :], a[name]).then_inc(const_in, 16)
            for g in range(GROUPS):
                sp.wait_ge(k_out, g + 1)
                sp.wait_ge(zeroed[g], 1)
                for hp in range(HP):
                    r = slice(hp * 2 * DK, (hp + 1) * 2 * DK)
                    c = slice(g * GC, (g + 1) * GC)
                    sp.dma_start(k_diag[r, hp, c], k_t[r, c]).then_inc(k_diag_in, 16)
            sp.dma_start(b1[:, :], a["b1"].partition_broadcast(P)).then_inc(ffn_in, 16)
            sp.dma_start(b2[:, :], a["b2"].partition_broadcast(P)).then_inc(ffn_in, 16)
            sp.dma_start(w1[:, :], a["w1"]).then_inc(ffn_in, 16)
            sp.dma_start(w2[:, :], a["w2"]).then_inc(ffn_in, 16)
            mid = x_mid.rearrange("(t p) w -> p t w", p=P)
            with sp.Fori(0, TILES) as t:
                sp.wait_ge(row_kept, t + 1)
                sp.wait_ge(row_done, t + 1)
                sp.dma_start(mid[:, ds(t, 1), :], rows[:, ds(t, 1), :]).then_inc(rows_out, 16)

        @block.tensor
        def _(pe):
            mm = nc.tensor.matmul

            def project_q(g):
                pe.wait_ge(xt_out, g + 1)
                after(pe, q_out, g - 1)
                mm(bank[6 + g % 2][:, :], wq[:, :], q_t[:, g * GC:(g + 1) * GC], start=True, stop=True).then_inc(q_done, 1)

            k_banks = (0, 1, 2, 5)
            pe.wait_ge(wk_in, 16)
            pe.wait_ge(ctx_in, 16)
            for g in range(GROUPS):
                mm(bank[k_banks[g]][:, :], wk[:, :], ctx_t[:, g * GC:(g + 1) * GC], start=True, stop=True).then_inc(k_done, 1)
            pe.wait_ge(w_in, 5 * 16)
            for g in range(GROUPS):
                after(pe, v_out0, 4 * (g - 1))
                after(pe, v_out1, 4 * (g - 1))
                for i in range(GT):
                    t = g * GT + i
                    last = mm(bank[3 + g % 2][:, i * D:(i + 1) * D], ctx_t[:, t * P:(t + 1) * P], wv[:, :], start=True, stop=True)
                last.then_inc(v_done, 1)
            for g in range(GROUPS):
                pe.wait_ge(xn_done, (g + 1) * GT)
                pe.wait_ge(k_out, g + 1)
                for i in range(GT):
                    last = nc.tensor.transpose(bank[k_banks[g]][:, i * P:(i + 1) * P], xn[:, g * GT + i, :], ident[:, :])
                last.then_inc(xt_done, 1)
                if g:
                    project_q(g - 1)
            project_q(GROUPS - 1)
            pe.wait_ge(k_diag_in, GROUPS * HP * 16)
            pe.wait_ge(v_fixed, 1)
            pe.wait_ge(q_out, GROUPS)
            pe.wait_ge(v_out0, 4 * GROUPS)
            pe.wait_ge(v_out1, 4 * GROUPS)

            def half_step(p, j):
                b = 2 * p + j
                if valid(b, B):
                    pe.wait_ge(q_par_done, b + 1)
                    after(pe, sub_done, b - 1)
                    mm(bank[j][:, :], q_par[:, j, :, :], k_diag[:, :, ds(b * S, S)], start=True, stop=True).then_inc(s_done, 1)
                if valid(b - 1, B):
                    pe.wait_ge(sub_done, b)
                    after(pe, exp_done, b - 2)
                    for c in range(C):
                        last = nc.tensor.transpose(bank[3 - j][:, c * P:(c + 1) * P], s_sub[:, 1 - j, c * P:(c + 1) * P], ident[:, :])
                    last.then_inc(st_done, 1)
                if valid(b - 2, B):
                    pe.wait_ge(exp_done, b - 1)
                    if j == 0:
                        after(pe, o_done, p - 1)
                    else:
                        pe.wait_ge(v_now_done, p)
                    for c in range(C):
                        for m in range(2):
                            n = 2 * c + m
                            last = mm(bank[4][j * S:(j + 1) * S, n * VC:(n + 1) * VC], p_t[:, j, n * S:(n + 1) * S],
                                      v_now[:, c, m, :] if j else v_diag[:, ds(b - 2, 1), c, m, :], start=True, stop=True)
                    last.then_inc(pv_done, 1)

            def iteration(p):
                half_step(p, 0)
                if valid(p - 2, TILES):
                    pe.wait_ge(o_done, p - 1)
                    after(pe, ot_out, p - 2)
                    nc.tensor.transpose(bank[6][:, 0:P], o_sb[:, :], ident[:, :]).then_inc(ot_done, 1)
                if valid(p - LAG_ROUTE, TILES):
                    pe.wait_ge(x2t_out, p - LAG_ROUTE + 1)
                    mm(bank[5][:, P:P + E], xn2_t[:, :], wr[:, :], start=True, stop=True).then_inc(route_done, 1)
                half_step(p, 1)
                if valid(p - 2, TILES):
                    pe.wait_ge(ot_out, p - 1)
                    after(pe, xm_done, p - 2)
                    mm(bank[7][:, 0:D], o_t[:, :], wo[:, :], start=True, stop=True).then_inc(proj_done, 1)
                if valid(p - LAG_XM, TILES):
                    pe.wait_ge(xn2_done, p - LAG_XM + 1)
                    after(pe, logit_done, p - LAG_XM)
                    nc.tensor.transpose(bank[5][:, 0:P], xn2[:, :], ident[:, :]).then_inc(x2t_done, 1)
                if at(p, TILES + 1):
                    count(0, EARLY)
                if at(p, TILES + 2):
                    mark(0, EARLY)

            def count(t0, t1):
                pe.wait_ge(onehot_done, 1 if t0 == 0 else 2)
                out = bank[0][:, 0:(TILES + 1) * E].rearrange("p (t e) -> p t e", e=E)
                last_t = TILES - 1
                mm(out[:, t0:t1, :], tri[:, :], onehot[:, t0:t1, :], start=t0 == 0, stop=False, skip_group_check=True)
                for t in range(t0, t1):
                    n = TILES - t
                    last = mm(out[:, t + 1:TILES + 1, :], ones[:, :], onehot[:, t:t + 1, :].to_broadcast([P, n, E]),
                              start=False, stop=t == last_t, skip_group_check=True)
                last.then_inc(rank_done, 1)

            def mark(t0, t1):
                pe.wait_ge(places_done, 1 if t0 == 0 else 2)
                for t in range(t0, t1):
                    last = mm(bank[1][0:CODES, 0:P], where_code[:, t, :], where_pos[:, t, :], start=t == 0, stop=t == TILES - 1)
                if t1 == TILES:
                    last.then_inc(table_done, 1)

            pipeline(pe, iteration, PEEL, TILES, ATT_END)

            count(EARLY, TILES)
            mark(EARLY, TILES)
            pe.wait_ge(table_out, 1)
            pe.wait_ge(jobs_done, 1)
            mm(bank[2][:, 0:JC], table[:, :], pick[:, :], start=True, stop=True).then_inc(slots_done, 1)

            pe.wait_ge(ffn_in, 4 * 16)
            pe.wait_ge(jobs_done, 1)
            pe.wait_ge(index_done, 1)

            def expert_of(j):
                return pe.value_load(job_i[0:1, ds(j, 1)], min_val=0, max_val=E - 1)

            def transpose_x(q, n):
                j, k = q * NG + n, n % 2
                pe.wait_ge(xf_done, j + 1)
                after(pe, xft_out, j - 1)
                nc.tensor.transpose(bank[6 + k][:, 0:P], xf[:, k, :], ident[:, :]).then_inc(xft_done, 1)

            def up(q, n):
                j, k = q * NG + n, n % 2
                pe.wait_ge(xft_out, j + 1)
                after(pe, hid_done, j - 1)
                mm(bank[k][:, :], xf_t[:, k, :], w1[:, ds(expert[n] * F, F)], start=True, stop=True).then_inc(h_done, 1)

            def transpose_h(q, n):
                j, k = q * NG + n, n % 2
                pe.wait_ge(hid_done, j + 1)
                after(pe, gelu_done, j - 1)
                for c in range(FC):
                    last = nc.tensor.transpose(bank[2 + k][:, c * P:(c + 1) * P], hid[:, k, c * P:(c + 1) * P], ident[:, :])
                last.then_inc(ht_done, 1)

            def down(q, n):
                j, k = q * NG + n, n % 2
                e = expert[n]
                pe.wait_ge(gelu_done, j + 1)
                after(pe, yb_done, j - 1)
                for c in range(FC):
                    last = mm(bank[4 + k][:, 0:D], hid_t[:, k, c * P:(c + 1) * P], w2[:, ds(e * (FC * D) + c * D, D)],
                              start=c == 0, stop=c == FC - 1)
                last.then_inc(y_done, 1)

            expert = {}

            def load_experts(q, n):
                for m in (n - 1, n):
                    if has_job(q, m):
                        expert[m] = expert_of(q * NG + m)

            def do_job(q, n):
                up(q, n)
                if has_job(q, n - 1):
                    down(q, n - 1)
                if has_job(q, n + 2):
                    transpose_x(q, n + 2)
                if n not in LAST and has_job(q, n + 1):
                    expert[n + 1] = expert_of(q * NG + n + 1)
                transpose_h(q, n)

            LAST = (FIRST - 1, FIRST + NG - 1)
            transpose_x(0, 0)
            transpose_x(0, 1)
            all_jobs(pe, do_job, load_experts)
            down(0, JOBS - 1)

        @block.scalar
        def _(act):
            go = nc.scalar.activation
            act.wait_ge(zero_set, 1)
            go(k_diag[:, :, 0:GC], zero[:, 0:1].unsqueeze(2).to_broadcast([P, HP, GC]), ACT.Copy).then_inc(zeroed[0], 1)
            k_banks = (0, 1, 2, 5)
            for g in range(GROUPS):
                act.wait_ge(k_done, g + 1)
                go(k_t[:, g * GC:(g + 1) * GC], bank[k_banks[g]][:, :], ACT.Copy).then_inc(k_out, 1)
            for g in range(GROUPS):
                act.wait_ge(v_done, g + 1)
                for half in range(2):
                    for par in range(2):
                        go(*place_v(g, 1, half, par), ACT.Copy).then_inc(v_out1, 1)

            def move_q(g):
                act.wait_ge(q_done, g + 1)
                go(q_t[:, g * GC:(g + 1) * GC], bank[6 + g % 2][:, :], ACT.Copy).then_inc(q_out, 1)

            for g in range(GROUPS):
                act.wait_ge(xt_done, g + 1)
                go(q_t[:, g * GC:(g + 1) * GC], bank[k_banks[g]][:, :], ACT.Copy).then_inc(xt_out, 1)
                if g:
                    move_q(g - 1)
            move_q(GROUPS - 1)

            def exps(b, j):
                act.wait_ge(st_done, b + 1)
                after(act, pv_done, b - 1)
                go(p_t[:, j, :], bank[2 + j][:, :], ACT.Exp, scale=float(DK) ** -0.5).then_inc(exp_done, 1)

            def iteration(p):
                if valid(2 * p - 1, B):
                    exps(2 * p - 1, 1)
                if valid(p - 2, TILES):
                    act.wait_ge(ot_done, p - 1)
                    after(act, proj_done, p - 2)
                    go(o_t[:, :], bank[6][:, 0:P], ACT.Copy).then_inc(ot_out, 1)
                if valid(2 * p, B):
                    exps(2 * p, 0)
                if valid(p - LAG_XM, TILES):
                    act.wait_ge(x2t_done, p - LAG_XM + 1)
                    after(act, route_done, p - LAG_XM)
                    go(xn2_t[:, :], bank[5][:, 0:P], ACT.Copy).then_inc(x2t_out, 1)
                if valid(p - LAG_ROUTE, TILES):
                    t = p - LAG_ROUTE
                    after(act, gsum_done, t)
                    act.wait_ge(logit_done, t + 1)
                    go(gexp[:, :], logit[:, ds(t, 1), :].rearrange("p a e -> p (a e)"), ACT.Exp,
                       accum_out=gsum[:, ds(t, 1)]).then_inc(gsum_done, 1)

            pipeline(act, iteration, PEEL, TILES, ATT_END)

            def move_x(q, n):
                j, k = q * NG + n, n % 2
                act.wait_ge(xft_done, j + 1)
                after(act, h_done, j - 1)
                go(xf_t[:, k, :], bank[6 + k][:, 0:P], ACT.Copy).then_inc(xft_out, 1)

            def gelu(q, n):
                j, k = q * NG + n, n % 2
                act.wait_ge(ht_done, j + 1)
                after(act, y_done, j - 1)
                go(hid_t[:, k, :], bank[2 + k][:, :], ACT.Gelu).then_inc(gelu_done, 1)

            def do_job(q, n):
                if has_job(q, n + 2):
                    move_x(q, n + 2)
                gelu(q, n)

            act.wait_ge(table_done, 1)
            go(table[:, :], bank[1][0:CODES, 0:P], ACT.Copy).then_inc(table_out, 1)
            move_x(0, 0)
            move_x(0, 1)
            all_jobs(act, do_job, lambda q, n: None)

        @block.vector
        def _(dve):
            v = nc.vector
            v.memset(k_diag[:, :, GC:2 * GC], 0.0).then_inc(zeroed[1], 1)
            for g in range(GROUPS):
                dve.wait_ge(x_in[g], 16)
                for t in range(g * GT, (g + 1) * GT):
                    v.bn_stats(stats[:, t, :], rows[:, t, 0:D]).then_inc(stats_done, 1)
            dve.wait_ge(stats_done, TILES)
            for t in range(TILES):
                v.bn_aggr(moments[:, t, :], stats[:, t, :]).then_inc(moments_done, 1)

            def move_v(g):
                dve.wait_ge(v_done, g + 1)
                for half in range(2):
                    for par in range(2):
                        v.tensor_copy(*place_v(g, 0, half, par)).then_inc(v_out0, 1)

            move_v(0)
            move_v(1)
            dve.wait_ge(rstd1_done, 1)
            for t in range(TILES):
                v.tensor_scalar(xn[:, t, :], rows[:, t, 0:D], moments[:, t, 0:1], rstd1[:, t:t + 1],
                                ALU.subtract, ALU.mult).then_inc(xn_done, 1)
            move_v(2)
            move_v(3)

            weighted = bank[4][:, 0:2 * C * VC].rearrange("p (n w) -> p n w", w=VC)

            def largest(b, j):
                dve.wait_ge(s_done, b + 1)
                v.reduce_max(s_max[:, j, :], bank[j][:, :].rearrange("p (h k) -> p h k", h=HP), AX.X).then_inc(max_done, 1)

            def shift(b, j):
                dve.wait_ge(max_done, b + 1)
                after(dve, st_done, b - 1)
                v.tensor_tensor(s_sub[:, j, :].rearrange("p (h k) -> p h k", h=HP), bank[j][:, :].rearrange("p (h k) -> p h k", h=HP),
                                s_max[:, j, :].unsqueeze(2).to_broadcast([P, HP, S]), ALU.subtract).then_inc(sub_done, 1)

            def iteration(p):
                o, m, r, w = p - 2, p - LAG_XM, p - LAG_ROUTE, p - LAG_ROW
                if valid(o, TILES):
                    dve.wait_ge(pv_done, 2 * (o + 1))
                    v.reciprocal(den[:, :, :], weighted[:, :, 2 * DK:VC]).then_inc(den_done, 1)
                if valid(m, TILES):
                    dve.wait_ge(proj_done, m + 1)
                    after(dve, row_kept, m)
                    v.tensor_tensor(row[:, 0:D], bank[7][:, 0:D], rows[:, ds(m, 1), 0:D].rearrange("p a d -> p (a d)"), ALU.add).then_inc(xm_done, 1)
                if valid(o, TILES):
                    dve.wait_ge(den_done, o + 1)
                    after(dve, ot_done, o)
                    v.tensor_tensor(o_sb[:, :].rearrange("p (n m d) -> p n m d", n=2 * C, m=2),
                                    weighted[:, :, 0:2 * DK].rearrange("p n (m d) -> p n m d", m=2),
                                    den[:, :, :].unsqueeze(3).to_broadcast([P, 2 * C, 2, DK]), ALU.mult).then_inc(o_done, 1)
                if valid(2 * p, B):
                    largest(2 * p, 0)
                if valid(m, TILES):
                    dve.wait_ge(xm_done, m + 1)
                    v.bn_stats(stats2[:, :], row[:, 0:D]).then_inc(stats2_done, 1)
                if valid(2 * p, B):
                    shift(2 * p, 0)
                if valid(m, TILES):
                    dve.wait_ge(stats2_done, m + 1)
                    dve.sem_inc(dve_met, 1)
                    v.bn_aggr(row[:, MEAN:VAR + 1], stats2[:, :]).then_inc(moments2_done, 1)
                if at(p, TILES):
                    choose(0, EARLY)
                if valid(w, TILES):
                    dve.wait_ge(gsum_done, w + 1)
                    v.reciprocal(rows[:, ds(w, 1), TOP:RW].rearrange("p a d -> p (a d)"), gsum[:, ds(w, 1)]).then_inc(row_done, 1)
                if valid(r, TILES):
                    dve.wait_ge(route_done, r + 1)
                    v.reduce_max(top[:, :], bank[5][:, P:P + E], AX.X).then_inc(top_done, 1)
                if valid(2 * p + 1, B):
                    largest(2 * p + 1, 1)
                if valid(r, TILES):
                    dve.wait_ge(top_done, r + 1)
                    v.tensor_scalar(logit[:, ds(r, 1), :].rearrange("p a e -> p (a e)"), bank[5][:, P:P + E],
                                    top[:, :], None, ALU.subtract).then_inc(logit_done, 1)
                if valid(2 * p + 1, B):
                    shift(2 * p + 1, 1)
                if at(p, TILES + 1):
                    locate(0, EARLY)
                if at(p, TILES + 2):
                    place(0, EARLY)

            steps = [0]

            def then(ins):
                steps[0] += 1
                ins.then_inc(step, 1)
                dve.wait_ge(step, steps[0])

            def choose(t0, t1):
                n = t1 - t0
                dve.wait_ge(logit_done, t1)
                if t0 == 0:
                    dve.wait_ge(const_in, len(CONSTS) * 16)
                t = slice(t0, t1)
                then(v.scalar_tensor_tensor(cand[:, t, :], logit[:, t, :], 0.0, first[:, :].unsqueeze(1).to_broadcast([P, n, E]),
                                            ALU.is_ge, ALU.mult))
                then(v.reduce_max(best[:, t], cand[:, t, :], AX.X))
                v.tensor_tensor(onehot[:, t, :], cand[:, t, :], best[:, t].unsqueeze(2).to_broadcast([P, n, E]), ALU.is_equal).then_inc(onehot_done, 1)

            def locate(t0, t1):
                n, t = t1 - t0, slice(t0, t1)
                dve.wait_ge(rank_done, 1 if t0 == 0 else 2)
                dve.wait_ge(onehot_done, 1 if t0 == 0 else 2)
                then(v.tensor_tensor(ranked[:, t, :], bank[0][:, t0 * E:t1 * E].rearrange("p (t e) -> p t e", e=E), onehot[:, t, :], ALU.mult))
                then(v.reduce_sum(rank[:, t], ranked[:, t, :], AX.X))
                then(v.tensor_copy(rank_i[:, t], rank[:, t]))
                then(v.tensor_single_scalar(slot_i[:, t], rank_i[:, t], 7, ALU.arith_shift_right))
                v.scalar_tensor_tensor(pos[:, t], slot_i[:, t], -float(P), rank[:, t], ALU.mult, ALU.add)
                then(v.scalar_tensor_tensor(code[:, t], best[:, t], -float(SLOTS), slot_i[:, t], ALU.mult, ALU.add))

            def place(t0, t1):
                for t in range(t0, t1):
                    v.tensor_scalar(where_pos[:, t, :], position[:, :], pos[:, t:t + 1], None, ALU.is_equal)
                    last = v.tensor_scalar(where_code[:, t, :], code_row[:, :], code[:, t:t + 1], token1[:, t:t + 1], ALU.is_equal, ALU.mult)
                last.then_inc(places_done, 1)

            pipeline(dve, iteration, PEEL, TILES, ATT_END)

            choose(EARLY, TILES)
            locate(EARLY, TILES)
            place(EARLY, TILES)
            then(v.tensor_single_scalar(cnt_i[:, 0, :], bank[0][:, TILES * E:(TILES + 1) * E], float(P - 1), ALU.add))
            then(v.tensor_single_scalar(cnt_i[:, 1, :], cnt_i[:, 0, :], 7, ALU.arith_shift_right))
            tiles_of = cnt_i[:, 1, :]
            then(v.tensor_tensor_scan(ends[:, :], tiles_of, tiles_of, 0.0, ALU.add, ALU.bypass))
            jobs = count_up[:, 0:JC]
            then(v.tensor_tensor(past[:, :, :], jobs.unsqueeze(2).to_broadcast([P, JC, E]),
                                 ends[:, :].unsqueeze(1).to_broadcast([P, JC, E]), ALU.is_ge))
            v.tensor_tensor(past_n[:, :, :], past[:, :, :], tiles_of.unsqueeze(1).to_broadcast([P, JC, E]), ALU.mult)
            then(v.reduce_sum(job[:, 0, :], past[:, :, :], AX.X))
            v.reduce_sum(job[:, 1, :], past_n[:, :, :], AX.X)
            then(v.scalar_tensor_tensor(job[:, 2, :], job[:, 0, :], float(SLOTS), jobs, ALU.mult, ALU.add))
            then(v.tensor_tensor(job[:, 3, :], job[:, 2, :], job[:, 1, :], ALU.subtract))
            v.tensor_single_scalar(job_i[:, :], job[:, 0, :], float(E - 1), ALU.min)
            v.tensor_scalar(pick[:, :], job[:, 3, :], partition[:, :], None, ALU.is_equal).then_inc(jobs_done, 1)
            dve.wait_ge(slots_done, 1)
            v.tensor_scalar(from_row[:, :], bank[2][:, 0:JC], -1.0, 0.0, ALU.add, ALU.max)
            then(v.tensor_scalar(empty[:, :], bank[2][:, 0:JC], 0.0, float(NOWHERE + 1), ALU.is_equal, ALU.mult))
            v.scalar_tensor_tensor(to_row[:, :], empty[:, :], -1.0, bank[2][:, 0:JC], ALU.add, ALU.add).then_inc(index_done, 1)

            def expert_of(j):
                return dve.value_load(job_i[0:1, ds(j, 1)], min_val=0, max_val=E - 1)

            def norm_x(q, n):
                j, k, g = q * NG + n, n % 2, n % NG
                dve.wait_ge(got[g], (q + n // NG + 1) * 16)
                after(dve, xft_done, j - 1)
                v.tensor_scalar(xf[:, k, :], gathered[:, g, 0:D], gathered[:, g, MEAN:MEAN + 1],
                                gathered[:, g, RSTD:RSTD + 1], ALU.subtract, ALU.mult).then_inc(xf_done, 1)

            def bias_h(q, n):
                j, k = q * NG + n, n % 2
                dve.wait_ge(h_done, j + 1)
                after(dve, ht_done, j - 1)
                v.tensor_tensor(hid[:, k, :], bank[k][:, :], b1[:, ds(expert[n] * F, F)], ALU.add).then_inc(hid_done, 1)

            def finish(q, n):
                j, k, g, r = q * NG + n, n % 2, n % NG, n % NR
                dve.wait_ge(y_done, j + 1)
                v.tensor_tensor(yb[:, k, :], bank[4 + k][:, 0:D], b2[:, ds(expert[n] * D, D)], ALU.add).then_inc(yb_done, 1)
                dve.wait_ge(yb_done, j + 1)
                after(dve, put[r], (q * (NG // NR) + n // NR) * 16)
                v.scalar_tensor_tensor(res[:, r, :], yb[:, k, :], gathered[:, g, TOP:RW], gathered[:, g, 0:D],
                                       ALU.mult, ALU.add).then_inc(res_done, 1)

            expert = {}

            def load_experts(q, n):
                for m in (n - 1, n):
                    if has_job(q, m):
                        expert[m] = expert_of(q * NG + m)

            def do_job(q, n):
                bias_h(q, n)
                if n not in LAST and has_job(q, n + 1):
                    expert[n + 1] = expert_of(q * NG + n + 1)
                if has_job(q, n - 1):
                    finish(q, n - 1)
                if has_job(q, n + 3):
                    norm_x(q, n + 3)

            LAST = (FIRST - 1, FIRST + NG - 1)
            dve.wait_ge(ffn_in, 4 * 16)
            for n in range(3):
                norm_x(0, n)
            all_jobs(dve, do_job, load_experts)
            finish(0, JOBS - 1)

        @block.gpsimd
        def _(pool):
            g_ = nc.gpsimd
            n_filled = [0]

            def alone(ins):
                n_filled[0] += 1
                ins.then_inc(filled, 1)
                pool.wait_ge(filled, n_filled[0])

            g_.memset(zero[:, :], 0.0).then_inc(zero_set, 1)
            alone(g_.memset(neg_half[:, :], -0.5))
            alone(g_.memset(eps[:, :], EPS))
            g_.memset(k_diag[:, :, 2 * GC:3 * GC], 0.0).then_inc(zeroed[2], 1)
            pool.wait_ge(moments_done, TILES)
            g_.tensor_tensor(rstd1[:, :], moments[:, :, 1], eps[:, :], ALU.add).then_inc(rstd1_in, 1)
            pool.wait_ge(rstd1_in, 1)
            g_.tensor_tensor(rstd1[:, :], rstd1[:, :], neg_half[:, :], ALU.pow).then_inc(rstd1_done, 1)
            g_.memset(k_diag[:, :, 3 * GC:4 * GC], 0.0).then_inc(zeroed[3], 1)
            pool.wait_ge(rstd1_done, 1)
            pool.wait_ge(zeroed[2], 1)
            pool.wait_ge(zeroed[3], 1)
            for h in range(2):
                r = slice(h * S, (h + 1) * S)
                alone(g_.memset(v_diag[r, :, :, :, (1 - h) * DK:(2 - h) * DK], 0.0))
                alone(g_.memset(v_diag[r, :, :, :, 2 * DK:VC], 0.0))
                alone(g_.memset(v_diag[r, :, :, :, 2 * DK + h:2 * DK + h + 1], 1.0))
            alone(g_.memset(ones[:, :], 1.0))
            pool.sem_inc(v_fixed, 1)
            pool.wait_ge(const_in, len(CONSTS) * 16)
            pool.wait_ge(q_out, GROUPS)

            def spread_q(b, j):
                after(pool, s_done, b - 1)
                pool.sem_inc(pool_met, 1)
                g_.tensor_tensor(q_par[:, j, :, :], q_t[:, ds(b * S, S)].unsqueeze(1).to_broadcast([P, 2, S]),
                                 parity[:, :].unsqueeze(2).to_broadcast([P, 2, S]), ALU.mult).then_inc(q_par_done, 1)

            def iteration(p):
                if valid(2 * p + 1, B):
                    spread_q(2 * p + 1, 1)
                if valid(2 * p - 1, B):
                    after(pool, pv_done, 2 * p - 2)
                    pool.sem_inc(pool_met, 1)
                    g_.tensor_copy(v_now[:, :, :, :], v_diag[:, ds(2 * p - 1, 1), :, :, :].rearrange("p a c m w -> p (a c) m w")).then_inc(v_now_done, 1)
                if valid(2 * p + 2, B):
                    spread_q(2 * p + 2, 0)
                if valid(p - LAG_XM, TILES):
                    t = p - LAG_XM
                    pool.wait_ge(moments2_done, t + 1)
                    g_.tensor_tensor(vare[:, :], row[:, VAR:RSTD], eps[:, 0:1], ALU.add).then_inc(vare_done, 1)
                    pool.wait_ge(vare_done, t + 1)
                    g_.tensor_tensor(row[:, RSTD:TOP], vare[:, :], neg_half[:, 0:1], ALU.pow).then_inc(rstd2_done, 1)
                    g_.tensor_tensor(xc[:, :], row[:, 0:D], row[:, MEAN:VAR].to_broadcast([P, D]), ALU.subtract).then_inc(rstd2_done, 1)
                    pool.wait_ge(rstd2_done, 2 * (t + 1))
                    after(pool, x2t_done, t)
                    g_.tensor_tensor(xn2[:, :], xc[:, :], row[:, RSTD:TOP].to_broadcast([P, D]), ALU.mult).then_inc(xn2_done, 1)
                    g_.tensor_copy(rows[:, ds(t, 1), 0:TOP].rearrange("p a d -> p (a d)"), row[:, 0:TOP]).then_inc(row_kept, 1)

            spread_q(0, 0)
            pipeline(pool, iteration, PEEL, TILES - 1, TILES + LAG_XM)

            pool.wait_ge(rows_out, TILES * 16)
            pool.wait_ge(index_done, 1)

            def copy_indices(q, n, now, row, s):
                g_.tensor_copy(now[:, n // NI % 2, :], row[:, ds(q * NG + n, NI)]).then_inc(s, 1)
                pool.wait_ge(s, q * (NG // NI) + n // NI + 1)
                pool.sem_inc(pool_met, 1)

            def gather(q, n):
                j, g = q * NG + n, n % NG
                if not (isinstance(q, int) and n < NG):
                    pool.wait_ge(res_done, j - NG + 1)
                    pool.sem_inc(pool_met, 1)
                if n % NI == 0:
                    copy_indices(q, n, from_now, from_row, from_done)
                g_.indirect_dma_start(out=gathered[:, g, :], out_offset=None, in_=x_mid,
                                      in_offset=bass.IndirectOffsetOnAxis(ap=from_now[:, n // NI % 2, n % NI:n % NI + 1].bitcast(u32), axis=0)).then_inc(got[g], 16)

            def scatter(q, n):
                j, r = q * NG + n, n % NR
                pool.wait_ge(res_done, j + 1)
                pool.sem_inc(pool_met, 1)
                if n % NI == 0:
                    copy_indices(q, n, to_now, to_row, to_done)
                g_.indirect_dma_start(out=a["out"], out_offset=bass.IndirectOffsetOnAxis(ap=to_now[:, n // NI % 2, n % NI:n % NI + 1].bitcast(u32), axis=0),
                                      in_=res[:, r, :], in_offset=None, bounds_check=TOK - 1, oob_is_err=False).then_inc(put[r], 16)

            def do_job(q, n):
                if has_job(q, n + AHEAD):
                    gather(q, n + AHEAD)
                if has_job(q, n - 2):
                    scatter(q, n - 2)

            for n in range(AHEAD):
                gather(0, n)
            all_jobs(pool, do_job, lambda q, n: None)
            scatter(0, JOBS - 2)
            scatter(0, JOBS - 1)
            for r in range(NR):
                pool.wait_ge(put[r], len(range(r, JOBS, NR)) * 16)

    return nc


_INS = ["x", "ctx_t", "wq", "wk", "wv", "wo", "wr", "w1", "b1", "w2", "b2",
        "ident", "parity", "tri", "first", "token1", "count_up", "position", "code_row", "partition"]


def kernel(x, ctx_768, L0_xattn_Wq, L0_xattn_Wk, L0_xattn_Wv, L0_xattn_Wo,
           L0_ffn_Wr, L0_ffn_W1, L0_ffn_b1, L0_ffn_W2, L0_ffn_b2):
    import concourse.bacc as bacc
    from concourse.bass_utils import run_bass_kernel_spmd

    c = np.ascontiguousarray
    data = {
        "x": c(np.asarray(x).reshape(TILES, P, D).transpose(1, 0, 2)).reshape(P, TILES * D),
        "ctx_t": c(np.asarray(ctx_768).reshape(TOK, KV).T),
        "wq": c(np.asarray(L0_xattn_Wq).T), "wk": c(np.asarray(L0_xattn_Wk).T),
        "wv": c(np.asarray(L0_xattn_Wv).T),
        "wo": c(np.asarray(L0_xattn_Wo).T.reshape(C, 2, 2, DK, D).transpose(0, 2, 1, 3, 4)).reshape(D, D),
        "wr": c(np.asarray(L0_ffn_Wr)),
        "w1": c(np.asarray(L0_ffn_W1).transpose(1, 0, 2)).reshape(D, E * F),
        "b1": c(np.asarray(L0_ffn_b1)).reshape(E * F),
        "w2": c(np.asarray(L0_ffn_W2).reshape(E, FC, P, D).transpose(2, 0, 1, 3)).reshape(P, E * FC * D),
        "b2": c(np.asarray(L0_ffn_b2)).reshape(E * D),
        "ident": np.eye(P, dtype=np.float32),
        "parity": c(((np.arange(P)[:, None] // DK) % 2 == np.arange(2)[None, :]).astype(np.float32)),
        "tri": np.triu(np.ones((P, P), np.float16), 1),
        "first": np.broadcast_to((E - np.arange(E)).astype(np.float32), (P, E)).copy(),
        "token1": (np.arange(P)[:, None] + P * np.arange(TILES)[None, :] + 1).astype(np.float32),
        "position": np.broadcast_to(np.arange(P, dtype=np.float16), (P, P)).copy(),
        "code_row": np.broadcast_to((np.arange(CODES) - CODES).astype(np.float16), (P, CODES)).copy(),
        "partition": np.arange(P, dtype=np.float32).reshape(P, 1),
        "count_up": np.broadcast_to(np.arange(P, dtype=np.float32), (P, P)).copy(),
    }
    nc = bacc.Bacc("TRN2", target_bir_lowering=False, num_devices=1)
    arrays, aps = {}, {}
    for name in _INS:
        arrays[f"in_{name}"] = data[name]
        aps[name] = nc.dram_tensor(f"in_{name}", data[name].shape, mybir.dt.from_np(data[name].dtype), kind="ExternalInput").ap()
    aps["out"] = nc.dram_tensor("out_x", [TOK, D], mybir.dt.float32, kind="ExternalOutput").ap()
    build(nc, aps)
    r = run_bass_kernel_spmd(nc, [arrays], core_ids=[0])
    return r.results[0]["out_x"].reshape(B, S, D)
```

```python
import numpy as np
from contextlib import ExitStack

import concourse.bass as bass
from concourse import mybir
from concourse.alu_op_type import AluOpType as ALU

B, S, D = 32, 64, 128
KV = 96
H = 16
DK = D // H
E, F = 8, 512
P = 128
TOK = B * S
TILES = TOK // P
GROUPS = 4
GB = B // GROUPS
GT = TILES // GROUPS
GC = TOK // GROUPS
HP = H // 2
C = HP // 2
VC = 2 * DK + 2
FC = F // P
RW = D + 4
MEAN, VAR, RSTD, TOP = D, D + 1, D + 2, D + 3
SLOTS = TILES
CODES = E * SLOTS
JOBS = TILES + E - 1
JC = JOBS + 1
EARLY = TILES - 4
EPS = 1e-5
KV_PARTS = {"wk": D, "wv": D, "ctx_t": TOK}
CONST_PARTS = {"ident": P, "wq": D, "wo": D, "wr": E, "parity": 2, "own_pair": 2, "first": E, "token1": TILES, "count_up": P, "earlier": E, "tile_of": 1}
CONST16_PARTS = {"tri": P, "position": P, "code_row": CODES}
NOWHERE = 4095


def build(nc, a):
    f32, f16, i32, u32 = mybir.dt.float32, mybir.dt.float16, mybir.dt.int32, mybir.dt.uint32
    ACT, AX = mybir.ActivationFunctionType, mybir.AxisListType
    ds = bass.ds
    ctx = ExitStack()
    with ctx:
        def sb(name, shape, dt=f32):
            return ctx.enter_context(nc.sbuf_tensor(name, shape, dt))

        def sem(name):
            return ctx.enter_context(nc.semaphore(name))

        parts = {}

        def packed(name, rows_, widths, dt=f32):
            whole, at_ = sb(name, [rows_, sum(widths.values())], dt), 0
            for part, w in widths.items():
                parts[part], at_ = whole[:, at_:at_ + w], at_ + w
            return whole

        kv_in = packed("kv_in", KV, KV_PARTS)
        wk, wv, ctx_t = parts["wk"], parts["wv"], parts["ctx_t"]
        consts = packed("consts", P, CONST_PARTS)
        ident, wq, wo, wr = parts["ident"], parts["wq"], parts["wo"], parts["wr"]
        parity = parts["parity"]
        own_pair = parts["own_pair"]
        first = parts["first"]
        token1 = parts["token1"]
        count_up = parts["count_up"]
        earlier = parts["earlier"]
        tile_of = parts["tile_of"]
        consts16 = packed("consts16", P, CONST16_PARTS, f16)
        tri = parts["tri"]
        position = parts["position"]
        code_row = parts["code_row"]
        rows = sb("rows", [P, TILES, RW])
        stats = sb("stats", [P, TILES, 6])
        moments = sb("moments", [P, TILES, 2])
        rstd1 = sb("rstd1", [P, TILES])
        still = sb("still", [P, 512], f16)
        zero, one = sb("zero", [P, 1]), sb("one", [P, 1])
        neg_half, eps = sb("neg_half", [P, TILES]), sb("eps", [P, TILES])
        q_t = sb("q_t", [D, TOK])
        k_t = sb("k_t", [D, TOK])
        k_diag = sb("k_diag", [D, HP, TOK])
        v_diag = sb("v_diag", [P, B, C, 2, VC])
        q_par = sb("q_par", [D, 2, 2, S])
        s_max = sb("s_max", [P, 2, HP])
        v_now = sb("v_now", [P, C, 2, VC])
        xn = sb("xn", [P, TILES, D])
        s_sub = sb("s_sub", [P, 2, HP * S])
        p_t = sb("p_t", [P, 2, HP * S])
        den = sb("den", [P, 2 * C, 2])
        o_sb = sb("o_sb", [P, D])
        o_t = sb("o_t", [D, P])
        stats2 = sb("stats2", [P, 6])
        vare = sb("vare", [P, 1])
        row = sb("row", [P, TOP])
        nshift = sb("nshift", [P, 1])
        xn2 = sb("xn2", [P, D])
        xn2_t = sb("xn2_t", [D, P])
        top = sb("top", [P, 1])
        logit = sb("logit", [P, TILES, E])
        gexp = sb("gexp", [P, E])
        gsum = sb("gsum", [P, TILES])
        ones = sb("ones", [P, P], f16)
        cand = sb("cand", [P, TILES, E])
        best = sb("best", [P, TILES])
        onehot = sb("onehot", [P, TILES, E], f16)
        ranked = sb("ranked", [P, TILES, E])
        rank_i = sb("rank_i", [P, TILES], i32)
        slot_i = sb("slot_i", [P, TILES], i32)
        neg_pos = sb("neg_pos", [P, TILES])
        code = sb("code", [P, TILES])
        where_pos = k_diag[:, 0, 0:TILES * P // 2].bitcast(f16).rearrange("p (t n) -> p t n", n=P)
        distance = k_diag[:, 1, 0:EARLY * P].rearrange("p (t n) -> p t n", n=P)
        where_code = k_diag[:, 0, TILES * P // 2:TILES * P].bitcast(f16).rearrange("p (t n) -> p t n", n=CODES)
        cnt_i = sb("cnt_i", [P, 2, E], i32)
        ends = sb("ends", [P, E])
        past = sb("past", [P, JC, E])
        before, begin = sb("before", [P, E]), sb("begin", [P, 1])
        job = sb("job", [P, JC])
        JW = 12
        JOB_TURNS = 4
        job_i = sb("job_i", [P, JOB_TURNS * JW], i32)
        pick = sb("pick", [CODES, JC])
        table = sb("table", [CODES, P])
        slots = sb("slots", [P, JC])
        empty = sb("empty", [P, JC])
        from_row = sb("from_row", [P, JC], i32)
        to_row = sb("to_row", [P, JC], i32)
        w1 = sb("w1", [D, E * (F + FC)])
        w1_now = sb("w1_now", [P, 2, F + FC])
        w2 = sb("w2", [P, E * FC * D])
        b2 = sb("b2", [P, E * D])
        NG, NR, NI = 6, 3, 3
        OWN = 3
        gathered = sb("gathered", [P, OWN + NG, RW])
        from_now = sb("from_now", [P, OWN + NG], i32)
        to_now = sb("to_now", [P, 2, NI], i32)
        xf = sb("xf", [P, 2, D])
        xf_t = sb("xf_t", [D, 2, P])
        hid_t = k_diag[:, 2, 0:2 * F].rearrange("p (k n) -> p k n", k=2)
        yb = sb("yb", [P, 2, D])
        res = sb("res", [P, NR, D])

        bank = [ctx.enter_context(nc.psum_tensor(f"bank{i}", [P, 512], f32)) for i in range(8)]
        x_mid = nc.dram_tensor("x_mid", [TOK, RW], f32, kind="Internal").ap()

        const16_in, const_in, ffn_in = sem("const16_in"), sem("const_in"), sem("ffn_in")
        ctx_in = [sem("ctx_in0"), sem("ctx_in1")]
        x_in = [sem("x_in0"), sem("x_in1")]
        still_set, zero_set, filled = sem("still_set"), sem("zero_set"), sem("filled")
        zeroed = [sem("zeroed0"), sem("zeroed1"), sem("zeroed2")]
        v_fixed, k0_placed = sem("v_fixed"), sem("k0_placed")
        stats_done, moments_done, rstd1_in, rstd1_done, xn_done = (
            sem("stats_done"), sem("moments_done"), sem("rstd1_in"), sem("rstd1_done"), sem("xn_done"))
        k_done, v_done, xt_done, q_done = sem("k_done"), sem("v_done"), sem("xt_done"), sem("q_done")
        k_out, v_out0, v_out1, xt_out, q_out = (
            sem("k_out"), sem("v_out0"), sem("v_out1"), sem("xt_out"), sem("q_out"))
        k_diag_in = [sem("k_diag_in0"), sem("k_diag_in1")]
        v_now_done = sem("v_now_done")
        q_par_done, s_done, max_done, sub_done = sem("q_par_done"), sem("s_done"), sem("max_done"), sem("sub_done")
        st_done, exp_done, pv_done = sem("st_done"), sem("exp_done"), sem("pv_done")
        den_done, o_done, ot_done, ot_out, proj_done = (
            sem("den_done"), sem("o_done"), sem("ot_done"), sem("ot_out"), sem("proj_done"))
        xm_done, stats2_done, moments2_done, vare_done, rstd2_done, nshift_done, xn2_done = (
            sem("xm_done"), sem("stats2_done"), sem("moments2_done"), sem("vare_done"),
            sem("rstd2_done"), sem("nshift_done"), sem("xn2_done"))
        x2t_done, x2t_out, route_done, top_done, logit_done, gsum_done, row_done = (
            sem("x2t_done"), sem("x2t_out"), sem("route_done"), sem("top_done"),
            sem("logit_done"), sem("gsum_done"), sem("row_done"))
        row_kept, rows_out = sem("row_kept"), sem("rows_out")
        dve_met, pool_met = sem("dve_met"), sem("pool_met")
        step, step_done = sem("step"), sem("step_done")
        onehot_done, rank_done, located, distance_done, code_placed, pos_placed, table_done, table_out, pick_done, jobs_done, slots_done = (
            sem("onehot_done"), sem("rank_done"), sem("located"), sem("distance_done"), sem("code_placed"), sem("pos_placed"), sem("table_done"), sem("table_out"),
            sem("pick_done"), sem("jobs_done"), sem("slots_done"))
        from_done, to_done = sem("from_done"), sem("to_done")
        got = [sem(f"got{k}") for k in range(OWN + NG)]
        put = [sem(f"put{k}") for k in range(NR)]
        xf_done, xft_done, xft_out, w1_now_done, h_done, gelu_done, y_done, yb_done, res_done = (
            sem("xf_done"), sem("xft_done"), sem("xft_out"), sem("w1_now_done"), sem("h_done"),
            sem("gelu_done"), sem("y_done"), sem("yb_done"), sem("res_done"))

        def after(eng, s, n):
            if not (isinstance(n, int) and n <= 0):
                eng.wait_ge(s, n)

        def pipeline(eng, iteration, steady, loop_end, end):
            for i in range(steady):
                iteration(i)
            turns = (loop_end - steady) // 2
            with eng.Fori(0, turns) as i:
                iteration(2 * i + steady)
                iteration(2 * i + steady + 1)
            for i in range(steady + 2 * turns, end):
                iteration(i)

        def valid(i, n):
            return not isinstance(i, int) or 0 <= i < n

        def has_job(q, n):
            return not isinstance(q, int) or 0 <= n < JOBS

        FIRST = NR + 2
        AHEAD = 4

        def all_jobs(eng, do_job, at_start):
            for n in range(FIRST):
                do_job(0, n)
            turns = (JOBS - FIRST - AHEAD) // NG
            with eng.Fori(0, turns) as q:
                at_start(q, FIRST)
                for n in range(FIRST, FIRST + NG):
                    do_job(q, n)
            at_start(0, FIRST + turns * NG)
            for n in range(FIRST + turns * NG, JOBS):
                do_job(0, n)

        def buffer_of(n):
            return n if n < OWN else OWN + (n - OWN) % NG

        def times_used(q, n):
            return 1 if n < OWN else q + (n - OWN) // NG + 1

        def experts_of(engine, q, n):
            turn, m0 = (0, 0) if n == 0 else ((n - FIRST) // NG + 1, n - 2)
            _, e = nc.values_load_multi_w_load_instructions(
                job_i[0:1, ds((q + turn) * JW, NG + 3)], engines=[engine], min_val=0, max_val=E - 1,
                skip_runtime_bounds_check_because="they are counts, so not negative, and the minimum with E - 1 is taken")
            return {m0 + i: e[i] for i in range(NG + 3)}

        def at(i, n):
            return isinstance(i, int) and i == n

        LAG_XM, LAG_X2T, LAG_ROUTE, LAG_ROW = 3, 4, 5, 6
        PEEL, ATT_END = LAG_ROW, TILES + LAG_ROW

        KV_BANKS = ((0, 3), (1, 4), (2, 5), (7, 6))
        XT_BANKS = (0, 7, 5, 7)
        Q_BANKS = (1, 7, 5, 5)

        def place_v(g, m, half, par):
            n = g * GB + m
            dst = v_diag[half * S:(half + 1) * S, n:n + GB - 1:2, :, par, half * DK:(half + 1) * DK]
            src = bank[KV_BANKS[g][1]][m * S:(m + 1) * S, :].rearrange("p (t c m h d) -> p t c m h d", t=GT, m=2, h=2, d=DK)[:, :, :, half, par, :]
            return dst, src

        def keep_clock(n):
            for _ in range(n):
                nc.tensor.matmul(bank[6][:, :], still[:, 0:P], still[:, :], start=True, stop=True)

        block = ctx.enter_context(nc.Block())

        @block.sync
        def _(sp):
            xr = a["x"].rearrange("p (t d) -> p t d", d=D)
            sp.dma_start(kv_in[:, 0:2 * D + GC], a["kv_in"][:, 0:2 * D + GC]).then_inc(ctx_in[0], 16)
            sp.dma_start(consts[:, :], a["consts"]).then_inc(const_in, 16)
            sp.dma_start(rows[:, 0:2 * GT, 0:D], xr[:, 0:2 * GT, :]).then_inc(x_in[0], 16)
            sp.dma_start(kv_in[:, 2 * D + GC:], a["kv_in"][:, 2 * D + GC:]).then_inc(ctx_in[1], 16)
            sp.dma_start(rows[:, 2 * GT:, 0:D], xr[:, 2 * GT:, :]).then_inc(x_in[1], 16)

            def place_k(g0, g1, s):
                for hp in range(HP):
                    r = slice(hp * 2 * DK, (hp + 1) * 2 * DK)
                    c = slice(g0 * GC, g1 * GC)
                    sp.dma_start(k_diag[r, hp, c], k_t[r, c]).then_inc(s, 16)

            sp.wait_ge(k_out, 1)
            sp.wait_ge(zeroed[1], 1)
            place_k(1, 2, k_diag_in[0])
            sp.dma_start(consts16[:, :], a["consts16"]).then_inc(const16_in, 16)
            sp.wait_ge(k_out, GROUPS - 1)
            sp.wait_ge(zeroed[2], HP)
            place_k(2, GROUPS, k_diag_in[1])
            sp.dma_start(b2[:, :], a["b2"].partition_broadcast(P)).then_inc(ffn_in, 16)
            sp.dma_start(w1[:, :], a["w1"]).then_inc(ffn_in, 16)
            sp.dma_start(w2[:, :], a["w2"]).then_inc(ffn_in, 16)
            mid = x_mid.rearrange("(t p) w -> p t w", p=P)
            with sp.Fori(0, TILES) as t:
                sp.wait_ge(row_kept, t + 1)
                sp.wait_ge(row_done, t + 1)
                sp.dma_start(mid[:, ds(t, 1), :], rows[:, ds(t, 1), :]).then_inc(rows_out, 16)

        @block.tensor
        def _(pe):
            mm = nc.tensor.matmul

            def project_kv(g, k_bank, v_bank):
                mm(bank[k_bank][:, :], wk[:, :], ctx_t[:, g * GC:(g + 1) * GC], start=True, stop=True).then_inc(k_done, 1)
                for i in range(GT):
                    t = g * GT + i
                    last = mm(bank[v_bank][:, i * D:(i + 1) * D], ctx_t[:, t * P:(t + 1) * P], wv[:, :], start=True, stop=True)
                last.then_inc(v_done, 1)

            def transpose_xn(g, b):
                pe.wait_ge(xn_done, (g + 1) * GT)
                for i in range(GT):
                    last = nc.tensor.transpose(bank[b][:, i * P:(i + 1) * P], xn[:, g * GT + i, :], ident[:, :])
                last.then_inc(xt_done, 1)

            def project_q(g, b):
                pe.wait_ge(xt_out, g + 1)
                mm(bank[b][:, :], wq[:, :], q_t[:, g * GC:(g + 1) * GC], start=True, stop=True).then_inc(q_done, 1)

            def v_moved(groups):
                pe.wait_ge(v_out0, 4 * groups)
                pe.wait_ge(v_out1, 4 * groups)

            pe.wait_ge(still_set, 1)
            keep_clock(8)
            pe.wait_ge(ctx_in[0], 16)
            project_kv(0, *KV_BANKS[0])
            pe.wait_ge(ctx_in[1], 16)
            for g in range(1, GROUPS):
                project_kv(g, *KV_BANKS[g])
            pe.wait_ge(const_in, 16)
            pe.wait_ge(k0_placed, 6)
            transpose_xn(0, XT_BANKS[0])
            pe.wait_ge(k_out, 1)
            project_q(0, Q_BANKS[0])

            def project_later(p, half):
                if at(p, 0) and half == 1:
                    pe.wait_ge(k_out, GROUPS - 1)
                    transpose_xn(1, XT_BANKS[1])
                if at(p, 1) and half == 0:
                    project_q(1, Q_BANKS[1])
                if at(p, 1) and half == 1:
                    v_moved(3)
                    transpose_xn(2, XT_BANKS[2])
                if at(p, 2) and half == 0:
                    project_q(2, Q_BANKS[2])
                    pe.wait_ge(q_out, 2)
                    transpose_xn(3, XT_BANKS[3])
                    v_moved(GROUPS)
                if at(p, 2) and half == 1:
                    pe.wait_ge(xt_out, 4)
                if at(p, 3) and half == 0:
                    pe.wait_ge(q_out, 3)
                    project_q(3, Q_BANKS[3])
                if at(p, 4) and half == 0:
                    pe.wait_ge(q_out, 4)

            def half_step(p, j):
                b = 2 * p + j
                if valid(b, B):
                    pe.wait_ge(q_par_done, b + 1)
                    mm(bank[j][:, :], q_par[:, j, :, :], k_diag[:, :, ds(b * S, S)], start=True, stop=True).then_inc(s_done, 1)
                if at(p, 0) and j == 1:
                    pe.wait_ge(k_out, 2)
                if at(p, 1) and j == 0:
                    v_moved(2)
                if valid(b - 1, B):
                    pe.wait_ge(sub_done, b)
                    for c in range(C):
                        last = nc.tensor.transpose(bank[3 - j][:, c * P:(c + 1) * P], s_sub[:, 1 - j, c * P:(c + 1) * P], ident[:, :])
                    last.then_inc(st_done, 1)
                if valid(b - 2, B):
                    pe.wait_ge(exp_done, b - 1)
                    if j == 0:
                        after(pe, o_done, p - 1)
                    else:
                        pe.wait_ge(v_now_done, p)
                    for c in range(C):
                        for m in range(2):
                            n = 2 * c + m
                            last = mm(bank[4][j * S:(j + 1) * S, n * VC:(n + 1) * VC], p_t[:, j, n * S:(n + 1) * S],
                                      v_now[:, c, m, :] if j else v_diag[:, ds(b - 2, 1), c, m, :], start=True, stop=True)
                    last.then_inc(pv_done, 1)

            def iteration(p):
                if at(p, GT):
                    pe.wait_ge(k_diag_in[0], HP * 16)
                if at(p, PEEL - 1):
                    pe.wait_ge(k_diag_in[1], HP * 16)
                half_step(p, 0)
                project_later(p, 0)
                if valid(p - 2, TILES):
                    if not valid(2 * p - 2, B):
                        pe.wait_ge(o_done, p - 1)
                    nc.tensor.transpose(bank[6][:, 0:P], o_sb[:, :], ident[:, :]).then_inc(ot_done, 1)
                if valid(p - 3, TILES):
                    pe.wait_ge(xm_done, p - 2)
                if valid(p - LAG_ROUTE, TILES):
                    pe.wait_ge(x2t_out, p - LAG_ROUTE + 1)
                    if not valid(p - 3, TILES):
                        pe.wait_ge(logit_done, p - LAG_ROUTE)
                    mm(bank[7][:, P:P + E], xn2_t[:, :], wr[:, :], start=True, stop=True).then_inc(route_done, 1)
                if valid(p - LAG_X2T, TILES):
                    pe.wait_ge(xn2_done, p - LAG_X2T + 1)
                    nc.tensor.transpose(bank[5][:, 0:P], xn2[:, :], ident[:, :]).then_inc(x2t_done, 1)
                half_step(p, 1)
                project_later(p, 1)
                if valid(p - 2, TILES):
                    pe.wait_ge(ot_out, p - 1)
                    after(pe, logit_done, p - LAG_ROUTE + 1)
                    mm(bank[7][:, 0:D], o_t[:, :], wo[:, :], start=True, stop=True).then_inc(proj_done, 1)
                if at(p, TILES):
                    count(0, EARLY)

            def count(t0, t1):
                pe.wait_ge(onehot_done, 1 if t0 == 0 else 2)
                out = bank[0][:, 0:(TILES + 1) * E].rearrange("p (t e) -> p t e", e=E)
                last_t = TILES - 1
                mm(out[:, t0:t1, :], tri[:, :], onehot[:, t0:t1, :], start=t0 == 0, stop=False, skip_group_check=True)
                for t in range(t0, t1):
                    n = TILES - t
                    last = mm(out[:, t + 1:TILES + 1, :], ones[:, :], onehot[:, t:t + 1, :].to_broadcast([P, n, E]),
                              start=False, stop=t == last_t, skip_group_check=True)
                last.then_inc(rank_done, 1)

            def mark(t0, t1):
                pe.wait_ge(code_placed, t1)
                pe.wait_ge(pos_placed, t1)
                for t in range(t0, t1):
                    last = mm(bank[1][0:CODES, 0:P], where_code[:, t, :], where_pos[:, t, :], start=t == 0, stop=t == TILES - 1)
                if t1 == TILES:
                    last.then_inc(table_done, 1)

            pipeline(pe, iteration, PEEL, TILES, ATT_END)

            count(EARLY, TILES)
            mark(0, EARLY)
            mark(EARLY, TILES)
            pe.wait_ge(table_out, 1)
            pe.wait_ge(pick_done, 1)
            mm(bank[2][:, 0:JC], table[:, :], pick[:, :], start=True, stop=True).then_inc(slots_done, 1)

            keep_clock(12)
            pe.wait_ge(ffn_in, 3 * 16)
            pe.wait_ge(jobs_done, 1)

            def transpose_x(q, n):
                j, k = q * NG + n, n % 2
                pe.wait_ge(xf_done, j + 1)
                nc.tensor.transpose(bank[6 + k][:, 0:P], xf[:, k, :], ident[:, :]).then_inc(xft_done, 1)

            def up(q, n):
                j, k = q * NG + n, n % 2
                pe.wait_ge(xft_out, j + 1)
                pe.wait_ge(w1_now_done, j + 1)
                for c in range(FC):
                    last = mm(bank[k][:, c * P:(c + 1) * P], w1_now[:, k, c * P:(c + 1) * P], xf_t[:, k, :], start=True, stop=True)
                last.then_inc(h_done, 1)

            def down(q, n):
                j, k = q * NG + n, n % 2
                e = expert[n]
                pe.wait_ge(gelu_done, j + 1)
                after(pe, yb_done, j - 1)
                for c in range(FC):
                    last = mm(bank[4 + k][:, 0:D], hid_t[:, k, c * P:(c + 1) * P], w2[:, ds(e * (FC * D) + c * D, D)],
                              start=c == 0, stop=c == FC - 1)
                last.then_inc(y_done, 1)

            expert = {}

            def load_experts(q, n):
                expert.update(experts_of(mybir.EngineType.PE, q, n))

            def do_job(q, n):
                up(q, n)
                if has_job(q, n + 1):
                    transpose_x(q, n + 1)
                if has_job(q, n - 1):
                    down(q, n - 1)

            transpose_x(0, 0)
            load_experts(0, 0)
            all_jobs(pe, do_job, load_experts)
            down(0, JOBS - 1)

        @block.scalar
        def _(act):
            go = nc.scalar.activation
            act.wait_ge(zero_set, 1)
            go(k_diag[:, :, 0:GC], zero[:, 0:1].unsqueeze(2).to_broadcast([P, HP, GC]), ACT.Copy).then_inc(zeroed[0], 1)
            act.wait_ge(k_done, 1)
            act.wait_ge(const_in, 16)
            act.wait_ge(zeroed[0], 1)
            for quarter in range(2):
                r = slice(quarter * 32, (quarter + 1) * 32)
                for m in range(2):
                    go(k_diag[r, 2 * quarter + m, 0:GC], bank[KV_BANKS[0][0]][r, :], ACT.Copy, scale=own_pair[r, m:m + 1]).then_inc(k0_placed, 1)
            for g in range(1, GROUPS):
                act.wait_ge(k_done, g + 1)
                go(k_t[:, g * GC:(g + 1) * GC], bank[KV_BANKS[g][0]][:, :], ACT.Copy).then_inc(k_out, 1)

            def move_v(g):
                act.wait_ge(v_done, g + 1)
                act.wait_ge(v_fixed, 1)
                for half in range(2):
                    for par in range(2):
                        go(*place_v(g, 1, half, par), ACT.Copy).then_inc(v_out1, 1)

            def move_xt(g):
                act.wait_ge(xt_done, g + 1)
                go(q_t[:, g * GC:(g + 1) * GC], bank[XT_BANKS[g]][:, :], ACT.Copy).then_inc(xt_out, 1)

            def move_q(g):
                act.wait_ge(q_done, g + 1)
                go(q_t[:, g * GC:(g + 1) * GC], bank[Q_BANKS[g]][:, :], ACT.Copy).then_inc(q_out, 1)

            move_xt(0)
            move_v(0)
            move_q(0)
            move_v(1)

            def exps(b, j):
                act.wait_ge(st_done, b + 1)
                go(p_t[:, j, :], bank[2 + j][:, :], ACT.Exp, scale=float(DK) ** -0.5).then_inc(exp_done, 1)

            def iteration(p):
                if valid(2 * p - 1, B):
                    exps(2 * p - 1, 1)
                if at(p, 1):
                    move_q(1)
                if at(p, 2):
                    move_q(2)
                    move_xt(3)
                if at(p, 3):
                    move_q(3)
                if valid(p - 2, TILES):
                    act.wait_ge(ot_done, p - 1)
                    go(o_t[:, :], bank[6][:, 0:P], ACT.Copy).then_inc(ot_out, 1)
                if valid(2 * p, B):
                    exps(2 * p, 0)
                if at(p, 0):
                    move_v(2)
                    move_xt(1)
                if at(p, 1):
                    move_v(3)
                    move_xt(2)
                if valid(p - LAG_X2T, TILES):
                    act.wait_ge(x2t_done, p - LAG_X2T + 1)
                    go(xn2_t[:, :], bank[5][:, 0:P], ACT.Copy).then_inc(x2t_out, 1)
                if valid(p - LAG_XM, TILES):
                    t = p - LAG_XM
                    act.wait_ge(nshift_done, t + 1)
                    go(xn2[:, :], row[:, 0:D], ACT.Identity, scale=row[:, RSTD:TOP], bias=nshift[:, :]).then_inc(xn2_done, 1)
                    go(rows[:, ds(t, 1), 0:TOP].rearrange("p a d -> p (a d)"), row[:, 0:TOP], ACT.Copy).then_inc(row_kept, 1)
                if valid(p - LAG_ROUTE, TILES):
                    t = p - LAG_ROUTE
                    after(act, gsum_done, t)
                    act.wait_ge(logit_done, t + 1)
                    go(gexp[:, :], logit[:, ds(t, 1), :].rearrange("p a e -> p (a e)"), ACT.Exp,
                       accum_out=gsum[:, ds(t, 1)]).then_inc(gsum_done, 1)
                if at(p, TILES + 3):
                    distances()

            def distances():
                act.wait_ge(located, 1)
                for t in range(EARLY):
                    go(distance[:, t, :], position[:, :], ACT.Square, bias=neg_pos[:, t:t + 1]).then_inc(distance_done, 1)

            def place_positions():
                act.wait_ge(distance_done, EARLY)
                go(where_pos[:, 0:EARLY, :], distance[:, :, :], ACT.Relu, scale=-1.0, bias=one[:, :]).then_inc(pos_placed, EARLY)

            pipeline(act, iteration, PEEL, TILES, ATT_END)
            place_positions()

            def move_x(q, n):
                j, k = q * NG + n, n % 2
                act.wait_ge(xft_done, j + 1)
                after(act, h_done, j - 1)
                go(xf_t[:, k, :], bank[6 + k][:, 0:P], ACT.Copy).then_inc(xft_out, 1)

            def gelu(q, n):
                j, k = q * NG + n, n % 2
                act.wait_ge(h_done, j + 1)
                after(act, y_done, j - 1)
                for c in range(FC):
                    last = go(hid_t[:, k, c * P:(c + 1) * P], bank[k][:, c * P:(c + 1) * P], ACT.Gelu, bias=w1_now[:, k, F + c:F + c + 1])
                last.then_inc(gelu_done, 1)

            def do_job(q, n):
                if has_job(q, n + 1):
                    move_x(q, n + 1)
                gelu(q, n)

            act.wait_ge(table_done, 1)
            go(table[:, :], bank[1][0:CODES, 0:P], ACT.Copy).then_inc(table_out, 1)
            move_x(0, 0)
            all_jobs(act, do_job, lambda q, n: None)

        @block.vector
        def _(dve):
            v = nc.vector
            v.memset(k_diag[:, :, GC:2 * GC], 0.0).then_inc(zeroed[1], 1)
            def measure(g):
                dve.wait_ge(x_in[g // 2], 16)
                tiles = range(g * GT, (g + 1) * GT)
                for t in tiles:
                    v.bn_stats(stats[:, t, :], rows[:, t, 0:D]).then_inc(stats_done, 1)
                dve.wait_ge(stats_done, (g + 1) * GT)
                for t in tiles:
                    v.bn_aggr(moments[:, t, :], stats[:, t, :]).then_inc(moments_done, 1)

            def normalise(g):
                dve.wait_ge(rstd1_done, g + 1)
                for t in range(g * GT, (g + 1) * GT):
                    v.tensor_scalar(xn[:, t, :], rows[:, t, 0:D], moments[:, t, 0:1], rstd1[:, t:t + 1],
                                    ALU.subtract, ALU.mult).then_inc(xn_done, 1)

            def move_v(g):
                dve.wait_ge(v_done, g + 1)
                dve.wait_ge(v_fixed, 1)
                for half in range(2):
                    for par in range(2):
                        v.tensor_copy(*place_v(g, 0, half, par)).then_inc(v_out0, 1)

            measure(0)
            dve.wait_ge(k_done, 1)
            dve.wait_ge(const_in, 16)
            dve.wait_ge(zeroed[0], 1)
            for quarter in range(2, 4):
                r = slice(quarter * 32, (quarter + 1) * 32)
                v.tensor_tensor(k_diag[r, 2 * quarter:2 * quarter + 2, 0:GC], bank[KV_BANKS[0][0]][r, :].unsqueeze(1).to_broadcast([32, 2, GC]),
                                own_pair[r, :].unsqueeze(2).to_broadcast([32, 2, GC]), ALU.mult).then_inc(k0_placed, 1)
            normalise(0)
            measure(1)
            move_v(0)
            normalise(1)
            move_v(1)
            measure(2)
            measure(3)

            weighted = bank[4][:, 0:2 * C * VC].rearrange("p (n w) -> p n w", w=VC)

            def largest(b, j):
                dve.wait_ge(s_done, b + 1)
                v.reduce_max(s_max[:, j, :], bank[j][:, :].rearrange("p (h k) -> p h k", h=HP), AX.X).then_inc(max_done, 1)

            def shift(b, j):
                dve.wait_ge(max_done, b + 1)
                v.tensor_tensor(s_sub[:, j, :].rearrange("p (h k) -> p h k", h=HP), bank[j][:, :].rearrange("p (h k) -> p h k", h=HP),
                                s_max[:, j, :].unsqueeze(2).to_broadcast([P, HP, S]), ALU.subtract).then_inc(sub_done, 1)

            def iteration(p):
                o, m, r, w = p - 2, p - LAG_XM, p - LAG_ROUTE, p - LAG_ROW
                if valid(o, TILES):
                    dve.wait_ge(pv_done, 2 * (o + 1))
                    v.reciprocal(den[:, :, :], weighted[:, :, 2 * DK:VC]).then_inc(den_done, 1)
                if valid(m, TILES):
                    dve.wait_ge(proj_done, m + 1)
                    after(dve, row_kept, m)
                    v.tensor_tensor(row[:, 0:D], bank[7][:, 0:D], rows[:, ds(m, 1), 0:D].rearrange("p a d -> p (a d)"), ALU.add).then_inc(xm_done, 1)
                if valid(o, TILES):
                    dve.wait_ge(den_done, o + 1)
                    v.tensor_tensor(o_sb[:, :].rearrange("p (n m d) -> p n m d", n=2 * C, m=2),
                                    weighted[:, :, 0:2 * DK].rearrange("p n (m d) -> p n m d", m=2),
                                    den[:, :, :].unsqueeze(3).to_broadcast([P, 2 * C, 2, DK]), ALU.mult).then_inc(o_done, 1)
                if valid(2 * p, B):
                    largest(2 * p, 0)
                if valid(m, TILES):
                    dve.wait_ge(xm_done, m + 1)
                    v.bn_stats(stats2[:, :], row[:, 0:D]).then_inc(stats2_done, 1)
                if valid(2 * p, B):
                    shift(2 * p, 0)
                if valid(m, TILES):
                    dve.wait_ge(stats2_done, m + 1)
                    dve.sem_inc(dve_met, 1)
                    v.bn_aggr(row[:, MEAN:VAR + 1], stats2[:, :]).then_inc(moments2_done, 1)
                if valid(w, TILES):
                    dve.wait_ge(gsum_done, w + 1)
                    v.reciprocal(rows[:, ds(w, 1), TOP:RW].rearrange("p a d -> p (a d)"), gsum[:, ds(w, 1)]).then_inc(row_done, 1)
                if valid(r, TILES):
                    dve.wait_ge(route_done, r + 1)
                    v.reduce_max(top[:, :], bank[7][:, P:P + E], AX.X).then_inc(top_done, 1)
                if valid(2 * p + 1, B):
                    largest(2 * p + 1, 1)
                if valid(r, TILES):
                    dve.wait_ge(top_done, r + 1)
                    v.tensor_scalar(logit[:, ds(r, 1), :].rearrange("p a e -> p (a e)"), bank[7][:, P:P + E],
                                    top[:, :], None, ALU.subtract).then_inc(logit_done, 1)
                if at(p, TILES):
                    choose(0, EARLY)
                if valid(2 * p + 1, B):
                    shift(2 * p + 1, 1)
                if at(p, 0) or at(p, 1):
                    move_v(p + 2)
                    normalise(p + 2)
                if at(p, TILES + 1):
                    locate(0, EARLY)
                if at(p, TILES + 2):
                    place(0, 5)
                if at(p, TILES + 3):
                    place(5, 9)

            steps = [0]

            def then(ins):
                steps[0] += 1
                ins.then_inc(step, 1)
                dve.wait_ge(step, steps[0])

            def choose(t0, t1):
                n = t1 - t0
                dve.wait_ge(logit_done, t1)
                if t0 == 0:
                    dve.wait_ge(const_in, 16)
                    dve.wait_ge(const16_in, 16)
                t = slice(t0, t1)
                then(v.scalar_tensor_tensor(cand[:, t, :], logit[:, t, :], 0.0, first[:, :].unsqueeze(1).to_broadcast([P, n, E]),
                                            ALU.is_ge, ALU.mult))
                then(v.reduce_max(best[:, t], cand[:, t, :], AX.X))
                v.tensor_tensor(onehot[:, t, :], cand[:, t, :], best[:, t].unsqueeze(2).to_broadcast([P, n, E]), ALU.is_equal).then_inc(onehot_done, 1)

            def locate(t0, t1):
                n, t = t1 - t0, slice(t0, t1)
                dve.wait_ge(rank_done, 1 if t0 == 0 else 2)
                dve.wait_ge(onehot_done, 1 if t0 == 0 else 2)
                then(v.tensor_tensor(ranked[:, t, :], bank[0][:, t0 * E:t1 * E].rearrange("p (t e) -> p t e", e=E), onehot[:, t, :], ALU.mult))
                with nc.allow_low_precision(reason="whole numbers, summed in float32"):
                    then(v.reduce_sum(rank_i[:, t], ranked[:, t, :], AX.X))
                then(v.tensor_single_scalar(slot_i[:, t], rank_i[:, t], 7, ALU.arith_shift_right))
                v.scalar_tensor_tensor(neg_pos[:, t], slot_i[:, t], float(P), rank_i[:, t], ALU.mult, ALU.subtract).then_inc(located, 1)
                then(v.scalar_tensor_tensor(code[:, t], best[:, t], -float(SLOTS), slot_i[:, t], ALU.mult, ALU.add))

            def place(t0, t1):
                for t in range(t0, t1):
                    last = v.tensor_scalar(where_code[:, t, :], code_row[:, :], code[:, t:t + 1], token1[:, t:t + 1], ALU.is_equal, ALU.mult)
                last.then_inc(code_placed, t1 - t0)

            def place_positions(t0, t1):
                for t in range(t0, t1):
                    last = v.tensor_scalar(where_pos[:, t, :], position[:, :], neg_pos[:, t:t + 1], 0.0, ALU.add, ALU.is_equal)
                last.then_inc(pos_placed, t1 - t0)

            pipeline(dve, iteration, PEEL, TILES, ATT_END)

            choose(EARLY, TILES)
            place(9, EARLY)
            locate(EARLY, TILES)
            place(EARLY, TILES)
            place_positions(EARLY, TILES)
            then(v.tensor_single_scalar(cnt_i[:, 0, :], bank[0][:, TILES * E:(TILES + 1) * E], float(P - 1), ALU.add))
            then(v.tensor_single_scalar(cnt_i[:, 1, :], cnt_i[:, 0, :], 7, ALU.arith_shift_right))
            tiles_of = cnt_i[:, 1, :]
            then(v.tensor_tensor(before[:, :], tiles_of, earlier[:, :], ALU.mult))
            then(v.reduce_sum(begin[:, :], before[:, :], AX.X))
            jobs = count_up[:, 0:JC]
            v.tensor_scalar(pick[:, :], jobs, begin[:, :], tile_of[:, :], ALU.subtract, ALU.is_equal).then_inc(pick_done, 1)
            then(v.tensor_tensor_scan(ends[:, :], tiles_of, tiles_of, 0.0, ALU.add, ALU.bypass))
            then(v.tensor_tensor(past[:, :, :], jobs.unsqueeze(2).to_broadcast([P, JC, E]),
                                 ends[:, :].unsqueeze(1).to_broadcast([P, JC, E]), ALU.is_ge))
            dve.wait_ge(slots_done, 1)
            v.tensor_scalar(from_now[:, :], bank[2][:, 0:OWN + NG], -1.0, 0.0, ALU.add, ALU.max).then_inc(from_done, (OWN + NG) // NI)
            v.tensor_scalar(from_row[:, :], bank[2][:, 0:JC], -1.0, 0.0, ALU.add, ALU.max)
            then(v.reduce_sum(job[:, :], past[:, :, :], AX.X))
            for turn in range(JOB_TURNS):
                j0 = 0 if turn == 0 else FIRST - 2 + (turn - 1) * NG
                last = v.tensor_single_scalar(job_i[:, turn * JW:turn * JW + NG + 3], job[:, j0:j0 + NG + 3], float(E - 1), ALU.min)
            then(last)
            dve.sem_inc(jobs_done, 1)
            then(v.tensor_scalar(empty[:, :], bank[2][:, 0:JC], 0.0, float(NOWHERE + 1), ALU.is_equal, ALU.mult))
            then(v.scalar_tensor_tensor(to_row[:, :], empty[:, :], -1.0, bank[2][:, 0:JC], ALU.add, ALU.add))
            v.tensor_copy(to_now[:, :, :], to_row[:, 0:2 * NI].rearrange("p (k n) -> p k n", k=2)).then_inc(to_done, 2)

            def norm_x(q, n):
                j, k, g = q * NG + n, n % 2, buffer_of(n)
                dve.wait_ge(got[g], times_used(q, n) * 16)
                after(dve, xft_done, j - 1)
                v.tensor_scalar(xf[:, k, :], gathered[:, g, 0:D], gathered[:, g, MEAN:MEAN + 1],
                                gathered[:, g, RSTD:RSTD + 1], ALU.subtract, ALU.mult).then_inc(xf_done, 1)

            def copy_w1(q, n):
                j, k = q * NG + n, n % 2
                after(dve, gelu_done, j - 1)
                v.tensor_copy(w1_now[:, k, :], w1[:, ds(expert[n] * (F + FC), F + FC)]).then_inc(w1_now_done, 1)

            def finish(q, n):
                j, k, g, r = q * NG + n, n % 2, buffer_of(n), n % NR
                dve.wait_ge(y_done, j + 1)
                v.tensor_tensor(yb[:, k, :], bank[4 + k][:, 0:D], b2[:, ds(expert[n] * D, D)], ALU.add).then_inc(yb_done, 1)
                dve.wait_ge(yb_done, j + 1)
                after(dve, put[r], (q * (NG // NR) + n // NR) * 16)
                v.scalar_tensor_tensor(res[:, r, :], yb[:, k, :], gathered[:, g, TOP:RW], gathered[:, g, 0:D],
                                       ALU.mult, ALU.add).then_inc(res_done, 1)

            expert = {}

            def load_experts(q, n):
                expert.update(experts_of(mybir.EngineType.DVE, q, n))

            def do_job(q, n):
                if has_job(q, n - 2):
                    finish(q, n - 2)
                if has_job(q, n + 2):
                    norm_x(q, n + 2)
                if has_job(q, n + 1):
                    copy_w1(q, n + 1)
                m = n + 2 + NI
                if m % NI == 0 and has_job(q, m) and not (isinstance(q, int) and m < OWN + NG):
                    v.tensor_copy(from_now[:, buffer_of(m):buffer_of(m) + NI], from_row[:, ds(q * NG + m, NI)]).then_inc(from_done, 1)
                m = n - 1
                if m % NI == 0 and not (isinstance(q, int) and m < 2 * NI):
                    v.tensor_copy(to_now[:, m // NI % 2, :], to_row[:, ds(q * NG + m, NI)]).then_inc(to_done, 1)

            dve.wait_ge(ffn_in, 3 * 16)
            load_experts(0, 0)
            copy_w1(0, 0)
            for n in range(2):
                norm_x(0, n)
            all_jobs(dve, do_job, load_experts)
            finish(0, JOBS - 2)
            finish(0, JOBS - 1)

        @block.gpsimd
        def _(pool):
            g_ = nc.gpsimd
            n_filled = [0]

            def alone(ins):
                n_filled[0] += 1
                ins.then_inc(filled, 1)
                pool.wait_ge(filled, n_filled[0])

            g_.memset(still[:, :], 0.0).then_inc(still_set, 1)
            g_.memset(zero[:, :], 0.0).then_inc(zero_set, 1)
            alone(g_.memset(one[:, :], 1.0))
            alone(g_.memset(neg_half[:, :], -0.5))
            alone(g_.memset(eps[:, :], EPS))
            for h in range(2):
                r = slice(h * S, (h + 1) * S)
                alone(g_.memset(v_diag[r, :, :, :, (1 - h) * DK:(2 - h) * DK].rearrange("p b c m d -> p (b c m) d"), 0.0))
                alone(g_.memset(v_diag[r, :, :, :, 2 * DK:VC], 0.0))
                alone(g_.memset(v_diag[r, :, :, :, 2 * DK + h:2 * DK + h + 1], 1.0))
            alone(g_.memset(ones[:, :], 1.0))
            pool.sem_inc(v_fixed, 1)

            def invert(g):
                t = slice(g * GT, (g + 1) * GT)
                pool.wait_ge(moments_done, (g + 1) * GT)
                g_.tensor_tensor(rstd1[:, t], moments[:, t, 1], eps[:, t], ALU.add).then_inc(rstd1_in, 1)
                pool.wait_ge(rstd1_in, g + 1)
                g_.tensor_tensor(rstd1[:, t], rstd1[:, t], neg_half[:, t], ALU.pow).then_inc(rstd1_done, 1)

            def zero_k(hp):
                g_.memset(k_diag[:, hp, 2 * GC:GROUPS * GC], 0.0).then_inc(zeroed[2], 1)

            invert(0)
            zero_k(0)
            invert(1)
            pool.wait_ge(const_in, 16)
            pool.wait_ge(q_out, 1)

            def spread_q(b, j):
                after(pool, s_done, b - 1)
                pool.sem_inc(pool_met, 1)
                g_.tensor_tensor(q_par[:, j, :, :], q_t[:, ds(b * S, S)].unsqueeze(1).to_broadcast([P, 2, S]),
                                 parity[:, :].unsqueeze(2).to_broadcast([P, 2, S]), ALU.mult).then_inc(q_par_done, 1)

            def iteration(p):
                if valid(2 * p + 1, B):
                    spread_q(2 * p + 1, 1)
                if at(p, 1) or at(p, 2) or at(p, 3):
                    zero_k(2 * p)
                if at(p, 1):
                    pool.wait_ge(v_out1, 4)
                if at(p, GT + 1):
                    pool.wait_ge(v_out1, 4 * GROUPS)
                    pool.wait_ge(q_out, GROUPS)
                if valid(2 * p - 1, B):
                    after(pool, pv_done, 2 * p - 2)
                    pool.sem_inc(pool_met, 1)
                    g_.tensor_copy(v_now[:, :, :, :], v_diag[:, ds(2 * p - 1, 1), :, :, :].rearrange("p a c m w -> p (a c) m w")).then_inc(v_now_done, 1)
                if at(p, GT - 1):
                    pool.wait_ge(q_out, 2)
                if valid(2 * p + 2, B):
                    spread_q(2 * p + 2, 0)
                if at(p, 0) or at(p, 1):
                    invert(p + 2)
                if at(p, 0) or at(p, 1) or at(p, 2) or at(p, 3):
                    zero_k(2 * p + 1)
                if valid(p - LAG_XM, TILES):
                    t = p - LAG_XM
                    pool.wait_ge(moments2_done, t + 1)
                    g_.tensor_tensor(vare[:, :], row[:, VAR:RSTD], eps[:, 0:1], ALU.add).then_inc(vare_done, 1)
                    pool.wait_ge(vare_done, t + 1)
                    g_.tensor_tensor(row[:, RSTD:TOP], vare[:, :], neg_half[:, 0:1], ALU.pow).then_inc(rstd2_done, 1)
                    pool.wait_ge(rstd2_done, t + 1)
                    pool.sem_inc(pool_met, 1)
                    g_.tensor_scalar(nshift[:, :], row[:, MEAN:VAR], row[:, RSTD:TOP], -1.0, ALU.mult, ALU.mult).then_inc(nshift_done, 1)

            spread_q(0, 0)
            pipeline(pool, iteration, PEEL, TILES - 2, TILES + LAG_XM)

            pool.wait_ge(rows_out, TILES * 16)

            def gather(q, n):
                j, g = q * NG + n, buffer_of(n)
                if not (isinstance(q, int) and n < OWN + NG):
                    pool.wait_ge(res_done, j - NG + 1)
                if n % NI == 0:
                    pool.wait_ge(from_done, q * (NG // NI) + n // NI + 1)
                pool.sem_inc(pool_met, 1)
                g_.indirect_dma_start(out=gathered[:, g, :], out_offset=None, in_=x_mid,
                                      in_offset=bass.IndirectOffsetOnAxis(ap=from_now[:, g:g + 1].bitcast(u32), axis=0)).then_inc(got[g], 16)

            def scatter(q, n):
                j, r = q * NG + n, n % NR
                pool.wait_ge(res_done, j + 1)
                if n % NI == 0:
                    pool.wait_ge(to_done, q * (NG // NI) + n // NI + 1)
                pool.sem_inc(pool_met, 1)
                g_.indirect_dma_start(out=a["out"], out_offset=bass.IndirectOffsetOnAxis(ap=to_now[:, n // NI % 2, n % NI:n % NI + 1].bitcast(u32), axis=0),
                                      in_=res[:, r, :], in_offset=None, bounds_check=TOK - 1, oob_is_err=False).then_inc(put[r], 16)

            def do_job(q, n):
                if has_job(q, n + AHEAD) and n >= FIRST:
                    gather(q, n + AHEAD)
                if has_job(q, n - 2):
                    scatter(q, n - 2)

            for n in range(OWN + NG):
                gather(0, n)
            all_jobs(pool, do_job, lambda q, n: None)
            for n in range(JOBS - 2, JOBS):
                scatter(0, n)
            for r in range(NR):
                pool.wait_ge(put[r], len(range(r, JOBS, NR)) * 16)

    return nc


_INS = ["x", "kv_in", "consts", "consts16", "w1", "w2", "b2"]


def kernel(x, ctx_768, L0_xattn_Wq, L0_xattn_Wk, L0_xattn_Wv, L0_xattn_Wo,
           L0_ffn_Wr, L0_ffn_W1, L0_ffn_b1, L0_ffn_W2, L0_ffn_b2):
    import concourse.bacc as bacc
    from concourse.bass_utils import run_bass_kernel_spmd

    c = np.ascontiguousarray
    data = {
        "x": c(np.asarray(x).reshape(TILES, P, D).transpose(1, 0, 2)).reshape(P, TILES * D),
        "ctx_t": c(np.asarray(ctx_768).reshape(TOK, KV).T),
        "wq": c(np.asarray(L0_xattn_Wq).T), "wk": c(np.asarray(L0_xattn_Wk).T),
        "wv": c(np.asarray(L0_xattn_Wv).T),
        "wo": c(np.asarray(L0_xattn_Wo).T.reshape(C, 2, 2, DK, D).transpose(0, 2, 1, 3, 4)).reshape(D, D),
        "wr": c(np.asarray(L0_ffn_Wr)),
        "w1": c(np.concatenate([np.asarray(L0_ffn_W1).transpose(1, 0, 2),
                                np.asarray(L0_ffn_b1).reshape(E, FC, P).transpose(2, 0, 1)], axis=2)).reshape(D, E * (F + FC)),
        "w2": c(np.asarray(L0_ffn_W2).reshape(E, FC, P, D).transpose(2, 0, 1, 3)).reshape(P, E * FC * D),
        "b2": c(np.asarray(L0_ffn_b2)).reshape(E * D),
        "ident": np.eye(P, dtype=np.float32),
        "parity": c(((np.arange(P)[:, None] // DK) % 2 == np.arange(2)[None, :]).astype(np.float32)),
        "own_pair": c(((np.arange(P)[:, None] // (2 * DK)) % 2 == np.arange(2)[None, :]).astype(np.float32)),
        "tri": np.triu(np.ones((P, P), np.float16), 1),
        "first": np.broadcast_to((E - np.arange(E)).astype(np.float32), (P, E)).copy(),
        "token1": (np.arange(P)[:, None] + P * np.arange(TILES)[None, :] + 1).astype(np.float32),
        "position": np.broadcast_to(np.arange(P, dtype=np.float16), (P, P)).copy(),
        "code_row": np.broadcast_to((np.arange(CODES) - CODES).astype(np.float16), (P, CODES)).copy(),
        "earlier": (np.arange(E)[None, :] < np.arange(P)[:, None] // SLOTS).astype(np.float32),
        "tile_of": (np.arange(P) % SLOTS).astype(np.float32).reshape(P, 1),
        "count_up": np.broadcast_to(np.arange(P, dtype=np.float32), (P, P)).copy(),
    }
    for whole, names in (("kv_in", KV_PARTS), ("consts", CONST_PARTS), ("consts16", CONST16_PARTS)):
        data[whole] = np.concatenate([data[n] for n in names], axis=1)
    nc = bacc.Bacc("TRN2", target_bir_lowering=False, num_devices=1)
    arrays, aps = {}, {}
    for name in _INS:
        arrays[f"in_{name}"] = data[name]
        aps[name] = nc.dram_tensor(f"in_{name}", data[name].shape, mybir.dt.from_np(data[name].dtype), kind="ExternalInput").ap()
    aps["out"] = nc.dram_tensor("out_x", [TOK, D], mybir.dt.float32, kind="ExternalOutput").ap()
    build(nc, aps)
    r = run_bass_kernel_spmd(nc, [arrays], core_ids=[0])
    return r.results[0]["out_x"].reshape(B, S, D)
```

```python
import numpy as np
from contextlib import ExitStack

import concourse.bass as bass
from concourse import mybir
from concourse.alu_op_type import AluOpType as ALU

B, S, D = 32, 64, 128
KV = 96
H = 16
DK = D // H
E, F = 8, 512
P = 128
TOK = B * S
TILES = TOK // P
GROUPS = 4
GB = B // GROUPS
GT = TILES // GROUPS
GC = TOK // GROUPS
HP = H // 2
C = HP // 2
VC = 2 * DK + 2
FC = F // P
RW = D + 4
MEAN, VAR, RSTD, TOP = D, D + 1, D + 2, D + 3
SLOTS = TILES
CODES = E * SLOTS
JOBS = TILES + E - 1
JC = JOBS + 1
EARLY = TILES - 4
BY_ACT = 10
EPS = 1e-5
KV_PARTS = {"wk": D, "wv": D, "ctx_t": TOK}
CONST_PARTS = {"ident": P, "wq": D, "wo": D, "wr": E, "parity": 2, "own_pair": 2, "first": E, "token1": TILES, "count_up": P, "earlier": E, "tile_of": 1}
CONST16_PARTS = {"tri": P, "position": P, "code_row": CODES}
NOWHERE = 4095


def build(nc, a):
    f32, f16, i32, u32 = mybir.dt.float32, mybir.dt.float16, mybir.dt.int32, mybir.dt.uint32
    ACT, AX = mybir.ActivationFunctionType, mybir.AxisListType
    ds = bass.ds
    ctx = ExitStack()
    with ctx:
        def sb(name, shape, dt=f32):
            return ctx.enter_context(nc.sbuf_tensor(name, shape, dt))

        def sem(name):
            return ctx.enter_context(nc.semaphore(name))

        parts = {}

        def packed(name, rows_, widths, dt=f32):
            whole, at_ = sb(name, [rows_, sum(widths.values())], dt), 0
            for part, w in widths.items():
                parts[part], at_ = whole[:, at_:at_ + w], at_ + w
            return whole

        kv_in = packed("kv_in", KV, KV_PARTS)
        wk, wv, ctx_t = parts["wk"], parts["wv"], parts["ctx_t"]
        consts = packed("consts", P, CONST_PARTS)
        ident, wq, wo, wr = parts["ident"], parts["wq"], parts["wo"], parts["wr"]
        parity = parts["parity"]
        own_pair = parts["own_pair"]
        first = parts["first"]
        token1 = parts["token1"]
        count_up = parts["count_up"]
        earlier = parts["earlier"]
        tile_of = parts["tile_of"]
        consts16 = packed("consts16", P, CONST16_PARTS, f16)
        tri = parts["tri"]
        position = parts["position"]
        code_row = parts["code_row"]
        rows = sb("rows", [P, TILES, RW])
        stats = sb("stats", [P, TILES, 6])
        moments = sb("moments", [P, TILES, 2])
        rstd1 = sb("rstd1", [P, TILES])
        scratch = sb("scratch", [P, 1])
        still = sb("still", [P, 512], f16)
        zero, one = sb("zero", [P, 1]), sb("one", [P, 1])
        neg_half, eps = sb("neg_half", [P, TILES]), sb("eps", [P, TILES])
        q_t = sb("q_t", [D, TOK])
        k_t = sb("k_t", [D, TOK])
        k_diag = sb("k_diag", [D, HP, TOK])
        v_diag = sb("v_diag", [P, B, C, 2, VC])
        q_par = sb("q_par", [D, 2, 2, S])
        s_max = sb("s_max", [P, 2, HP])
        v_now = sb("v_now", [P, C, 2, VC])
        xn = sb("xn", [P, TILES, D])
        s_sub = sb("s_sub", [P, 2, HP * S])
        p_t = sb("p_t", [P, 2, HP * S])
        den = sb("den", [P, 2 * C, 2])
        o_sb = sb("o_sb", [P, D])
        o_t = sb("o_t", [D, P])
        stats2 = sb("stats2", [P, 6])
        vare = sb("vare", [P, 1])
        row = sb("row", [P, TOP])
        nshift = sb("nshift", [P, 1])
        xn2 = sb("xn2", [P, D])
        xn2_t = sb("xn2_t", [D, P])
        top = sb("top", [P, 1])
        logit = sb("logit", [P, TILES, E])
        gexp = sb("gexp", [P, E])
        gsum = sb("gsum", [P, TILES])
        ones = sb("ones", [P, P], f16)
        cand = sb("cand", [P, TILES, E])
        best = sb("best", [P, TILES])
        onehot = sb("onehot", [P, TILES, E], f16)
        ranked = sb("ranked", [P, TILES, E])
        rank_i = sb("rank_i", [P, TILES], i32)
        slot_i = sb("slot_i", [P, TILES], i32)
        neg_pos = sb("neg_pos", [P, TILES])
        code = sb("code", [P, TILES])
        where_pos = k_diag[:, 0, 0:TILES * P // 2].bitcast(f16).rearrange("p (t n) -> p t n", n=P)
        distance = k_diag[:, 1, 0:BY_ACT * P].rearrange("p (t n) -> p t n", n=P)
        where_code = k_diag[:, 0, TILES * P // 2:TILES * P].bitcast(f16).rearrange("p (t n) -> p t n", n=CODES)
        cnt_i = sb("cnt_i", [P, 2, E], i32)
        ends = sb("ends", [P, E])
        past = sb("past", [P, JC, E])
        before, begin = sb("before", [P, E]), sb("begin", [P, 1])
        job = sb("job", [P, JC])
        NG = 6
        FIRST = 5
        TURNS = (JOBS - FIRST - 2) // NG
        JW = -(-(NG + 3) // 4) * 4
        job_i = sb("job_i", [P, (TURNS + 2) * JW], i32)
        pick = sb("pick", [CODES, JC])
        table = sb("table", [CODES, P])
        empty = sb("empty", [P, JC])
        from_row = sb("from_row", [P, JC], i32)
        to_row = sb("to_row", [P, JC], i32)
        w1 = sb("w1", [D, E * (F + FC)])
        w1_now = sb("w1_now", [P, 2, F + FC])
        w2 = sb("w2", [P, E * FC * D])
        b2 = sb("b2", [P, E * D])
        OWN = 3
        gathered = sb("gathered", [P, JOBS, RW])
        xf = sb("xf", [P, 2, D])
        xf_t = sb("xf_t", [D, 2, P])
        hid_t = k_diag[:, 2, 0:2 * F].rearrange("p (k n) -> p k n", k=2)
        yb = sb("yb", [P, 2, D])
        res = sb("res", [P, NG, D])

        bank = [ctx.enter_context(nc.psum_tensor(f"bank{i}", [P, 512], f32)) for i in range(8)]
        x_mid = nc.dram_tensor("x_mid", [TOK, RW], f32, kind="Internal").ap()

        const16_in, const_in, ffn_in = sem("const16_in"), sem("const_in"), sem("ffn_in")
        ctx_in = [sem("ctx_in0"), sem("ctx_in1")]
        x_in = [sem("x_in0"), sem("x_in1")]
        still_set, zero_set, filled = sem("still_set"), sem("zero_set"), sem("filled")
        zeroed = [sem("zeroed0"), sem("zeroed1"), sem("zeroed2")]
        v_fixed, k0_placed = sem("v_fixed"), sem("k0_placed")
        stats_done, moments_done, rstd1_in, rstd1_done, xn_done = (
            sem("stats_done"), sem("moments_done"), sem("rstd1_in"), sem("rstd1_done"), sem("xn_done"))
        k_done, v_done, xt_done, q_done = sem("k_done"), sem("v_done"), sem("xt_done"), sem("q_done")
        k_out, v_out, xt_out, q_out = sem("k_out"), sem("v_out"), sem("xt_out"), sem("q_out")
        k_diag_in = [sem("k_diag_in0"), sem("k_diag_in1")]
        v_now_done = sem("v_now_done")
        q_par_done, s_done, max_done, sub_done = sem("q_par_done"), sem("s_done"), sem("max_done"), sem("sub_done")
        st_done, exp_done, pv_done = sem("st_done"), sem("exp_done"), sem("pv_done")
        den_done, o_done, ot_done, ot_out, proj_done = (
            sem("den_done"), sem("o_done"), sem("ot_done"), sem("ot_out"), sem("proj_done"))
        xm_done, stats2_done, moments2_done, vare_done, rstd2_done, nshift_done, xn2_done = (
            sem("xm_done"), sem("stats2_done"), sem("moments2_done"), sem("vare_done"),
            sem("rstd2_done"), sem("nshift_done"), sem("xn2_done"))
        x2t_done, x2t_out, route_done, top_done, logit_done, gsum_done, row_done = (
            sem("x2t_done"), sem("x2t_out"), sem("route_done"), sem("top_done"),
            sem("logit_done"), sem("gsum_done"), sem("row_done"))
        row_kept, rows_out = sem("row_kept"), sem("rows_out")
        dve_met, pool_met = sem("dve_met"), sem("pool_met")
        step = sem("step")
        onehot_done, rank_done, located, distance_done, code_placed, pos_placed = (
            sem("onehot_done"), sem("rank_done"), sem("located"), sem("distance_done"),
            sem("code_placed"), sem("pos_placed"))
        table_done, table_out, pick_done, jobs_done, slots_done = (
            sem("table_done"), sem("table_out"), sem("pick_done"), sem("jobs_done"), sem("slots_done"))
        from_done, to_done = sem("from_done"), sem("to_done")
        got = [sem(f"got{k}") for k in range(OWN + NG)]
        put = [sem(f"put{k}") for k in range(NG)]
        xf_done, xft_done, xft_out, w1_now_done, h_done, gelu_done, y_done, yb_done, res_done = (
            sem("xf_done"), sem("xft_done"), sem("xft_out"), sem("w1_now_done"), sem("h_done"),
            sem("gelu_done"), sem("y_done"), sem("yb_done"), sem("res_done"))

        def after(eng, s, n):
            if not (isinstance(n, int) and n <= 0):
                eng.wait_ge(s, n)

        def pipeline(eng, iteration, steady, loop_end, end):
            for i in range(steady):
                iteration(i)
            turns = (loop_end - steady) // 2
            with eng.Fori(0, turns) as i:
                iteration(2 * i + steady)
                iteration(2 * i + steady + 1)
            for i in range(steady + 2 * turns, end):
                iteration(i)

        def valid(i, n):
            return not isinstance(i, int) or 0 <= i < n

        def has_job(q, n):
            return not isinstance(q, int) or 0 <= n < JOBS

        def all_jobs(eng, do_job, at_start):
            for n in range(FIRST):
                do_job(0, n)
            with eng.Fori(0, TURNS) as q:
                at_start(q, FIRST)
                for n in range(FIRST, FIRST + NG):
                    do_job(q, n)
            at_start(0, FIRST + TURNS * NG)
            for n in range(FIRST + TURNS * NG, JOBS):
                do_job(0, n)

        def got_of(n):
            return got[n if n < OWN else OWN + (n - OWN) % NG]

        def gathers_by(q, n):
            return 1 if n < OWN else q + (n - OWN) // NG + 1

        def experts_of(engine, q, n):
            turn, m0 = (0, 0) if n == 0 else ((n - FIRST) // NG + 1, n - 2)
            _, e = nc.values_load_multi_w_load_instructions(
                job_i[0:1, ds((q + turn) * JW, NG + 3)], engines=[engine], min_val=0, max_val=E - 1,
                skip_runtime_bounds_check_because="they are counts, so not negative, and the minimum with E - 1 is taken")
            return {m0 + i: e[i] for i in range(NG + 3)}

        def at(i, n):
            return isinstance(i, int) and i == n

        LAG_XM, LAG_X2T, LAG_ROUTE, LAG_ROW = 3, 4, 5, 6
        PEEL, ATT_END = LAG_ROW, TILES + LAG_ROW

        K_BANKS, V_BANKS = (0, 1, 2, 7), (3, 4, 5, 6)
        XT_BANKS = (6, 7, 5, 7)
        Q_BANKS = (1, 7, 5, 5)

        def place_v(g, m, half, par):
            n = g * GB + m
            dst = v_diag[half * S:(half + 1) * S, n:n + GB - 1:2, :, par, half * DK:(half + 1) * DK]
            src = bank[V_BANKS[g]][m * S:(m + 1) * S, :].rearrange("p (t c m h d) -> p t c m h d", t=GT, m=2, h=2, d=DK)[:, :, :, half, par, :]
            return dst, src

        def keep_clock(n):
            for _ in range(n):
                nc.tensor.matmul(bank[6][:, :], still[:, 0:P], still[:, :], start=True, stop=True)

        block = ctx.enter_context(nc.Block())

        @block.sync
        def _(sp):
            xr = a["x"].rearrange("p (t d) -> p t d", d=D)
            sp.dma_start(kv_in[:, 0:2 * D + GC], a["kv_in"][:, 0:2 * D + GC]).then_inc(ctx_in[0], 16)
            sp.dma_start(rows[:, 0:GT, 0:D], xr[:, 0:GT, :]).then_inc(x_in[0], 16)
            sp.dma_start(consts[:, :], a["consts"]).then_inc(const_in, 16)
            sp.dma_start(kv_in[:, 2 * D + GC:], a["kv_in"][:, 2 * D + GC:]).then_inc(ctx_in[1], 16)
            sp.dma_start(rows[:, GT:, 0:D], xr[:, GT:, :]).then_inc(x_in[1], 16)

            def place_k(g0, g1, s):
                for hp in range(HP):
                    r = slice(hp * 2 * DK, (hp + 1) * 2 * DK)
                    c = slice(g0 * GC, g1 * GC)
                    sp.dma_start(k_diag[r, hp, c], k_t[r, c]).then_inc(s, 16)

            sp.wait_ge(k_out, 1)
            sp.wait_ge(zeroed[1], 1)
            place_k(1, 2, k_diag_in[0])
            sp.dma_start(consts16[:, :], a["consts16"]).then_inc(const16_in, 16)
            sp.wait_ge(k_out, GROUPS - 1)
            sp.wait_ge(zeroed[2], HP)
            place_k(2, GROUPS, k_diag_in[1])
            sp.dma_start(b2[:, :], a["b2"].partition_broadcast(P)).then_inc(ffn_in, 16)
            sp.dma_start(w1[:, :], a["w1"]).then_inc(ffn_in, 16)
            sp.dma_start(w2[:, :], a["w2"]).then_inc(ffn_in, 16)
            mid = x_mid.rearrange("(t p) w -> p t w", p=P)
            with sp.Fori(0, TILES) as t:
                sp.wait_ge(row_kept, t + 1)
                sp.wait_ge(row_done, t + 1)
                sp.dma_start(mid[:, ds(t, 1), :], rows[:, ds(t, 1), :]).then_inc(rows_out, 16)

        @block.tensor
        def _(pe):
            mm = nc.tensor.matmul

            def project_k(g):
                mm(bank[K_BANKS[g]][:, :], wk[:, :], ctx_t[:, g * GC:(g + 1) * GC], start=True, stop=True).then_inc(k_done, 1)

            def project_v(g):
                for i in range(GT):
                    t = g * GT + i
                    last = mm(bank[V_BANKS[g]][:, i * D:(i + 1) * D], ctx_t[:, t * P:(t + 1) * P], wv[:, :], start=True, stop=True)
                last.then_inc(v_done, 1)

            def transpose_xn(g):
                b = XT_BANKS[g]
                pe.wait_ge(xn_done, (g + 1) * GT)
                for i in range(GT):
                    last = nc.tensor.transpose(bank[b][:, i * P:(i + 1) * P], xn[:, g * GT + i, :], ident[:, :])
                last.then_inc(xt_done, 1)

            def project_q(g):
                pe.wait_ge(xt_out, g + 1)
                mm(bank[Q_BANKS[g]][:, :], wq[:, :], q_t[:, g * GC:(g + 1) * GC], start=True, stop=True).then_inc(q_done, 1)

            def v_moved(groups):
                pe.wait_ge(v_out, 8 * groups)

            pe.wait_ge(still_set, 1)
            keep_clock(8)
            pe.wait_ge(ctx_in[0], 16)
            project_k(0)
            project_v(0)
            pe.wait_ge(ctx_in[1], 16)
            project_k(1)
            project_v(1)
            pe.wait_ge(const_in, 16)
            transpose_xn(0)
            project_k(2)
            pe.wait_ge(k_out, 1)
            project_q(0)
            project_v(2)
            project_k(3)
            pe.wait_ge(k0_placed, 6)
            pe.wait_ge(q_out, 1)

            def project_later(p, half):
                if at(p, 0) and half == 1:
                    pe.wait_ge(k_out, GROUPS - 1)
                    transpose_xn(1)
                if at(p, 1) and half == 0:
                    project_q(1)
                if at(p, 1) and half == 1:
                    v_moved(3)
                    transpose_xn(2)
                if at(p, 2) and half == 0:
                    project_q(2)
                    pe.wait_ge(q_out, 2)
                    transpose_xn(3)
                    v_moved(GROUPS)
                if at(p, 2) and half == 1:
                    pe.wait_ge(xt_out, 4)
                if at(p, 3) and half == 0:
                    pe.wait_ge(q_out, 3)
                    project_q(3)
                if at(p, 4) and half == 0:
                    pe.wait_ge(q_out, 4)

            def half_step(p, j):
                b = 2 * p + j
                if valid(b, B):
                    pe.wait_ge(q_par_done, b + 1)
                    mm(bank[j][:, :], q_par[:, j, :, :], k_diag[:, :, ds(b * S, S)], start=True, stop=True).then_inc(s_done, 1)
                if at(p, 0) and j == 1:
                    project_v(3)
                    pe.wait_ge(k_out, 2)
                if at(p, 1) and j == 0:
                    v_moved(2)
                if valid(b - 1, B):
                    pe.wait_ge(sub_done, b)
                    for c in range(C):
                        last = nc.tensor.transpose(bank[3 - j][:, c * P:(c + 1) * P], s_sub[:, 1 - j, c * P:(c + 1) * P], ident[:, :])
                    last.then_inc(st_done, 1)
                if valid(b - 2, B):
                    pe.wait_ge(exp_done, b - 1)
                    if j == 0:
                        after(pe, o_done, p - 1)
                    else:
                        pe.wait_ge(v_now_done, p)
                    for c in range(C):
                        for m in range(2):
                            n = 2 * c + m
                            last = mm(bank[4][j * S:(j + 1) * S, n * VC:(n + 1) * VC], p_t[:, j, n * S:(n + 1) * S],
                                      v_now[:, c, m, :] if j else v_diag[:, ds(b - 2, 1), c, m, :], start=True, stop=True)
                    last.then_inc(pv_done, 1)

            def iteration(p):
                if at(p, GT):
                    pe.wait_ge(k_diag_in[0], HP * 16)
                if at(p, PEEL - 1):
                    pe.wait_ge(k_diag_in[1], HP * 16)
                half_step(p, 0)
                project_later(p, 0)
                if valid(p - 2, TILES):
                    if not valid(2 * p - 2, B):
                        pe.wait_ge(o_done, p - 1)
                    nc.tensor.transpose(bank[6][:, 0:P], o_sb[:, :], ident[:, :]).then_inc(ot_done, 1)
                if valid(p - 3, TILES):
                    pe.wait_ge(xm_done, p - 2)
                if valid(p - LAG_ROUTE, TILES):
                    pe.wait_ge(x2t_out, p - LAG_ROUTE + 1)
                    if not valid(p - 3, TILES):
                        pe.wait_ge(logit_done, p - LAG_ROUTE)
                    mm(bank[7][:, P:P + E], xn2_t[:, :], wr[:, :], start=True, stop=True).then_inc(route_done, 1)
                if valid(p - LAG_X2T, TILES):
                    pe.wait_ge(xn2_done, p - LAG_X2T + 1)
                    nc.tensor.transpose(bank[5][:, 0:P], xn2[:, :], ident[:, :]).then_inc(x2t_done, 1)
                half_step(p, 1)
                project_later(p, 1)
                if valid(p - 2, TILES):
                    pe.wait_ge(ot_out, p - 1)
                    after(pe, logit_done, p - LAG_ROUTE + 1)
                    mm(bank[7][:, 0:D], o_t[:, :], wo[:, :], start=True, stop=True).then_inc(proj_done, 1)
                if at(p, TILES):
                    count(0, EARLY)

            def count(t0, t1):
                pe.wait_ge(onehot_done, 1 if t0 == 0 else 2)
                out = bank[0][:, 0:(TILES + 1) * E].rearrange("p (t e) -> p t e", e=E)
                last_t = TILES - 1
                mm(out[:, t0:t1, :], tri[:, :], onehot[:, t0:t1, :], start=t0 == 0, stop=False, skip_group_check=True)
                for t in range(t0, t1):
                    n = TILES - t
                    last = mm(out[:, t + 1:TILES + 1, :], ones[:, :], onehot[:, t:t + 1, :].to_broadcast([P, n, E]),
                              start=False, stop=t == last_t, skip_group_check=True)
                last.then_inc(rank_done, 1)

            def mark(t0, t1):
                pe.wait_ge(code_placed, t1)
                pe.wait_ge(pos_placed, t1)
                for t in range(t0, t1):
                    last = mm(bank[1][0:CODES, 0:P], where_code[:, t, :], where_pos[:, t, :], start=t == 0, stop=t == TILES - 1)
                if t1 == TILES:
                    last.then_inc(table_done, 1)

            pipeline(pe, iteration, PEEL, TILES, ATT_END)

            count(EARLY, TILES)
            mark(0, EARLY)
            mark(EARLY, TILES)
            pe.wait_ge(table_out, 1)
            pe.wait_ge(pick_done, 1)
            mm(bank[2][:, 0:JC], table[:, :], pick[:, :], start=True, stop=True).then_inc(slots_done, 1)

            keep_clock(9)
            pe.wait_ge(ffn_in, 3 * 16)
            pe.wait_ge(jobs_done, 1)

            def transpose_x(q, n):
                j, k = q * NG + n, n % 2
                pe.wait_ge(xf_done, j + 1)
                nc.tensor.transpose(bank[6 + k][:, 0:P], xf[:, k, :], ident[:, :]).then_inc(xft_done, 1)

            def up(q, n):
                j, k = q * NG + n, n % 2
                pe.wait_ge(xft_out, j + 1)
                pe.wait_ge(w1_now_done, j + 1)
                for c in range(FC):
                    last = mm(bank[k][:, c * P:(c + 1) * P], w1_now[:, k, c * P:(c + 1) * P], xf_t[:, k, :], start=True, stop=True)
                last.then_inc(h_done, 1)

            def down(q, n):
                j, k = q * NG + n, n % 2
                e = expert[n]
                pe.wait_ge(gelu_done, j + 1)
                after(pe, yb_done, j - 1)
                for c in range(FC):
                    last = mm(bank[4 + k][:, 0:D], hid_t[:, k, c * P:(c + 1) * P], w2[:, ds(e * (FC * D) + c * D, D)],
                              start=c == 0, stop=c == FC - 1)
                last.then_inc(y_done, 1)

            expert = {}

            def load_experts(q, n):
                expert.update(experts_of(mybir.EngineType.PE, q, n))

            def do_job(q, n):
                up(q, n)
                if has_job(q, n + 1):
                    transpose_x(q, n + 1)
                if has_job(q, n - 1):
                    down(q, n - 1)

            transpose_x(0, 0)
            load_experts(0, 0)
            all_jobs(pe, do_job, load_experts)
            down(0, JOBS - 1)

        @block.scalar
        def _(act):
            go = nc.scalar.activation
            act.wait_ge(zero_set, 1)
            go(k_diag[:, :, 0:GC], zero[:, 0:1].unsqueeze(2).to_broadcast([P, HP, GC]), ACT.Copy).then_inc(zeroed[0], 1)
            act.wait_ge(k_done, 1)
            act.wait_ge(const_in, 16)
            act.wait_ge(zeroed[0], 1)
            for quarter in range(2):
                r = slice(quarter * 32, (quarter + 1) * 32)
                for m in range(2):
                    go(k_diag[r, 2 * quarter + m, 0:GC], bank[K_BANKS[0]][r, :], ACT.Copy, scale=own_pair[r, m:m + 1]).then_inc(k0_placed, 1)

            def move_k(g):
                act.wait_ge(k_done, g + 1)
                go(k_t[:, g * GC:(g + 1) * GC], bank[K_BANKS[g]][:, :], ACT.Copy).then_inc(k_out, 1)

            def move_v(g):
                act.wait_ge(v_done, g + 1)
                act.wait_ge(v_fixed, 1)
                for m in range(2):
                    for half in range(2):
                        for par in range(2):
                            go(*place_v(g, m, half, par), ACT.Copy).then_inc(v_out, 1)

            def move_xt(g):
                act.wait_ge(xt_done, g + 1)
                go(q_t[:, g * GC:(g + 1) * GC], bank[XT_BANKS[g]][:, :], ACT.Copy).then_inc(xt_out, 1)

            def move_q(g):
                act.wait_ge(q_done, g + 1)
                go(q_t[:, g * GC:(g + 1) * GC], bank[Q_BANKS[g]][:, :], ACT.Copy).then_inc(q_out, 1)

            move_k(1)
            move_xt(0)
            move_v(0)
            move_k(2)
            move_q(0)
            move_k(3)
            move_v(1)

            def exps(b, j):
                act.wait_ge(st_done, b + 1)
                go(p_t[:, j, :], bank[2 + j][:, :], ACT.Exp, scale=float(DK) ** -0.5).then_inc(exp_done, 1)

            def iteration(p):
                if valid(2 * p - 1, B):
                    exps(2 * p - 1, 1)
                if at(p, 1):
                    move_q(1)
                if at(p, 2):
                    move_q(2)
                    move_xt(3)
                if at(p, 3):
                    move_q(3)
                if valid(p - 2, TILES):
                    act.wait_ge(ot_done, p - 1)
                    go(o_t[:, :], bank[6][:, 0:P], ACT.Copy).then_inc(ot_out, 1)
                if valid(2 * p, B):
                    exps(2 * p, 0)
                if at(p, 0):
                    move_xt(1)
                    move_v(2)
                if at(p, 1):
                    move_v(3)
                    move_xt(2)
                if valid(p - LAG_X2T, TILES):
                    act.wait_ge(x2t_done, p - LAG_X2T + 1)
                    go(xn2_t[:, :], bank[5][:, 0:P], ACT.Copy).then_inc(x2t_out, 1)
                if valid(p - LAG_XM, TILES):
                    t = p - LAG_XM
                    act.wait_ge(nshift_done, t + 1)
                    go(xn2[:, :], row[:, 0:D], ACT.Identity, scale=row[:, RSTD:TOP], bias=nshift[:, :]).then_inc(xn2_done, 1)
                    go(rows[:, ds(t, 1), 0:TOP].rearrange("p a d -> p (a d)"), row[:, 0:TOP], ACT.Copy).then_inc(row_kept, 1)
                if valid(p - LAG_ROUTE, TILES):
                    t = p - LAG_ROUTE
                    after(act, gsum_done, t)
                    act.wait_ge(logit_done, t + 1)
                    go(gexp[:, :], logit[:, ds(t, 1), :].rearrange("p a e -> p (a e)"), ACT.Exp,
                       accum_out=gsum[:, ds(t, 1)]).then_inc(gsum_done, 1)
                if at(p, TILES + 1):
                    distances(0, 4)
                if at(p, TILES + 3):
                    distances(4, BY_ACT)

            def distances(t0, t1):
                act.wait_ge(located, 1)
                for t in range(t0, t1):
                    go(distance[:, t, :], position[:, :], ACT.Square, bias=neg_pos[:, t:t + 1]).then_inc(distance_done, 1)

            def place_positions():
                act.wait_ge(distance_done, BY_ACT)
                go(where_pos[:, 0:BY_ACT, :], distance[:, :, :], ACT.Relu, scale=-1.0, bias=one[:, :]).then_inc(pos_placed, BY_ACT)

            pipeline(act, iteration, PEEL, TILES, ATT_END)
            place_positions()

            def move_x(q, n):
                j, k = q * NG + n, n % 2
                act.wait_ge(xft_done, j + 1)
                after(act, h_done, j - 1)
                go(xf_t[:, k, :], bank[6 + k][:, 0:P], ACT.Copy).then_inc(xft_out, 1)

            def gelu(q, n):
                j, k = q * NG + n, n % 2
                act.wait_ge(h_done, j + 1)
                after(act, y_done, j - 1)
                for c in range(FC):
                    last = go(hid_t[:, k, c * P:(c + 1) * P], bank[k][:, c * P:(c + 1) * P], ACT.Gelu, bias=w1_now[:, k, F + c:F + c + 1])
                last.then_inc(gelu_done, 1)

            def do_job(q, n):
                if has_job(q, n + 1):
                    move_x(q, n + 1)
                gelu(q, n)

            act.wait_ge(table_done, 1)
            go(table[:, :], bank[1][0:CODES, 0:P], ACT.Copy).then_inc(table_out, 1)
            go(scratch[:, :], one[:, :], ACT.Gelu)
            move_x(0, 0)
            all_jobs(act, do_job, lambda q, n: None)

        @block.vector
        def _(dve):
            v = nc.vector
            v.memset(k_diag[:, :, GC:2 * GC], 0.0).then_inc(zeroed[1], 1)

            def measure(g):
                dve.wait_ge(x_in[min(g, 1)], 16)
                tiles = range(g * GT, (g + 1) * GT)
                for t in tiles:
                    v.bn_stats(stats[:, t, :], rows[:, t, 0:D]).then_inc(stats_done, 1)
                dve.wait_ge(stats_done, (g + 1) * GT)
                for t in tiles:
                    v.bn_aggr(moments[:, t, :], stats[:, t, :]).then_inc(moments_done, 1)

            def normalise(g):
                dve.wait_ge(rstd1_done, g + 1)
                for t in range(g * GT, (g + 1) * GT):
                    v.tensor_scalar(xn[:, t, :], rows[:, t, 0:D], moments[:, t, 0:1], rstd1[:, t:t + 1],
                                    ALU.subtract, ALU.mult).then_inc(xn_done, 1)

            measure(0)
            dve.wait_ge(k_done, 1)
            dve.wait_ge(const_in, 16)
            dve.wait_ge(zeroed[0], 1)

            def place_k0(quarter):
                r = slice(quarter * 32, (quarter + 1) * 32)
                v.tensor_tensor(k_diag[r, 2 * quarter:2 * quarter + 2, 0:GC], bank[K_BANKS[0]][r, :].unsqueeze(1).to_broadcast([32, 2, GC]),
                                own_pair[r, :].unsqueeze(2).to_broadcast([32, 2, GC]), ALU.mult).then_inc(k0_placed, 1)

            place_k0(2)
            normalise(0)
            place_k0(3)
            measure(1)
            measure(2)
            normalise(1)

            weighted = bank[4][:, 0:2 * C * VC].rearrange("p (n w) -> p n w", w=VC)

            def largest(b, j):
                dve.wait_ge(s_done, b + 1)
                v.reduce_max(s_max[:, j, :], bank[j][:, :].rearrange("p (h k) -> p h k", h=HP), AX.X).then_inc(max_done, 1)

            def shift(b, j):
                dve.wait_ge(max_done, b + 1)
                v.tensor_tensor(s_sub[:, j, :].rearrange("p (h k) -> p h k", h=HP), bank[j][:, :].rearrange("p (h k) -> p h k", h=HP),
                                s_max[:, j, :].unsqueeze(2).to_broadcast([P, HP, S]), ALU.subtract).then_inc(sub_done, 1)

            def iteration(p):
                o, m, r, w = p - 2, p - LAG_XM, p - LAG_ROUTE, p - LAG_ROW
                if valid(o, TILES):
                    dve.wait_ge(pv_done, 2 * (o + 1))
                    v.reciprocal(den[:, :, :], weighted[:, :, 2 * DK:VC]).then_inc(den_done, 1)
                if valid(m, TILES):
                    dve.wait_ge(proj_done, m + 1)
                    after(dve, row_kept, m)
                    v.tensor_tensor(row[:, 0:D], bank[7][:, 0:D], rows[:, ds(m, 1), 0:D].rearrange("p a d -> p (a d)"), ALU.add).then_inc(xm_done, 1)
                if valid(o, TILES):
                    dve.wait_ge(den_done, o + 1)
                    v.tensor_tensor(o_sb[:, :].rearrange("p (n m d) -> p n m d", n=2 * C, m=2),
                                    weighted[:, :, 0:2 * DK].rearrange("p n (m d) -> p n m d", m=2),
                                    den[:, :, :].unsqueeze(3).to_broadcast([P, 2 * C, 2, DK]), ALU.mult).then_inc(o_done, 1)
                if valid(2 * p, B):
                    largest(2 * p, 0)
                if valid(m, TILES):
                    dve.wait_ge(xm_done, m + 1)
                    v.bn_stats(stats2[:, :], row[:, 0:D]).then_inc(stats2_done, 1)
                if valid(2 * p, B):
                    shift(2 * p, 0)
                if valid(m, TILES):
                    dve.wait_ge(stats2_done, m + 1)
                    dve.sem_inc(dve_met, 1)
                    v.bn_aggr(row[:, MEAN:VAR + 1], stats2[:, :]).then_inc(moments2_done, 1)
                if valid(w, TILES):
                    dve.wait_ge(gsum_done, w + 1)
                    v.reciprocal(rows[:, ds(w, 1), TOP:RW].rearrange("p a d -> p (a d)"), gsum[:, ds(w, 1)]).then_inc(row_done, 1)
                if valid(r, TILES):
                    dve.wait_ge(route_done, r + 1)
                    v.reduce_max(top[:, :], bank[7][:, P:P + E], AX.X).then_inc(top_done, 1)
                if valid(2 * p + 1, B):
                    largest(2 * p + 1, 1)
                if valid(r, TILES):
                    dve.wait_ge(top_done, r + 1)
                    v.tensor_scalar(logit[:, ds(r, 1), :].rearrange("p a e -> p (a e)"), bank[7][:, P:P + E],
                                    top[:, :], None, ALU.subtract).then_inc(logit_done, 1)
                if at(p, TILES):
                    choose(0, EARLY)
                if valid(2 * p + 1, B):
                    shift(2 * p + 1, 1)
                if at(p, 0):
                    normalise(2)
                    measure(3)
                if at(p, 1):
                    normalise(3)
                if at(p, TILES + 1):
                    locate()
                if at(p, TILES + 2):
                    place(0, 5)
                if at(p, TILES + 3):
                    place(5, 10)
                if at(p, TILES + 4):
                    choose(EARLY, TILES)

            steps = [0]

            def then(ins):
                steps[0] += 1
                ins.then_inc(step, 1)
                dve.wait_ge(step, steps[0])

            def choose(t0, t1):
                n = t1 - t0
                dve.wait_ge(logit_done, t1)
                if t0 == 0:
                    dve.wait_ge(const_in, 16)
                    dve.wait_ge(const16_in, 16)
                t = slice(t0, t1)
                then(v.scalar_tensor_tensor(cand[:, t, :], logit[:, t, :], 0.0, first[:, :].unsqueeze(1).to_broadcast([P, n, E]),
                                            ALU.is_ge, ALU.mult))
                then(v.reduce_max(best[:, t], cand[:, t, :], AX.X))
                v.tensor_tensor(onehot[:, t, :], cand[:, t, :], best[:, t].unsqueeze(2).to_broadcast([P, n, E]), ALU.is_equal).then_inc(onehot_done, 1)

            def locate():
                t = slice(0, EARLY)
                dve.wait_ge(rank_done, 1)
                dve.wait_ge(onehot_done, 1)
                then(v.tensor_tensor(ranked[:, t, :], bank[0][:, 0:EARLY * E].rearrange("p (t e) -> p t e", e=E), onehot[:, t, :], ALU.mult))
                with nc.allow_low_precision(reason="whole numbers, summed in float32"):
                    then(v.reduce_sum(rank_i[:, t], ranked[:, t, :], AX.X))
                then(v.tensor_single_scalar(slot_i[:, t], rank_i[:, t], 7, ALU.arith_shift_right))
                v.scalar_tensor_tensor(neg_pos[:, t], slot_i[:, t], float(P), rank_i[:, t], ALU.mult, ALU.subtract).then_inc(located, 1)
                then(v.scalar_tensor_tensor(code[:, t], best[:, t], -float(SLOTS), slot_i[:, t], ALU.mult, ALU.add))

            def place(t0, t1):
                for t in range(t0, t1):
                    last = v.tensor_scalar(where_code[:, t, :], code_row[:, :], code[:, t:t + 1], token1[:, t:t + 1], ALU.is_equal, ALU.mult)
                last.then_inc(code_placed, t1 - t0)

            def place_positions(t0, t1):
                for t in range(t0, t1):
                    last = v.tensor_scalar(where_pos[:, t, :], position[:, :], neg_pos[:, t:t + 1], 0.0, ALU.add, ALU.is_equal)
                last.then_inc(pos_placed, t1 - t0)

            pipeline(dve, iteration, PEEL, TILES, ATT_END)

            place(10, EARLY)
            place_positions(BY_ACT, EARLY)
            t = slice(EARLY, TILES)
            tiles_of = cnt_i[:, 1, :]
            dve.wait_ge(rank_done, 2)
            dve.wait_ge(onehot_done, 2)
            v.tensor_single_scalar(cnt_i[:, 0, :], bank[0][:, TILES * E:(TILES + 1) * E], float(P - 1), ALU.add)
            then(v.tensor_tensor(ranked[:, t, :], bank[0][:, EARLY * E:TILES * E].rearrange("p (t e) -> p t e", e=E), onehot[:, t, :], ALU.mult))
            v.tensor_single_scalar(cnt_i[:, 1, :], cnt_i[:, 0, :], 7, ALU.arith_shift_right)
            with nc.allow_low_precision(reason="whole numbers, summed in float32"):
                then(v.reduce_sum(rank_i[:, t], ranked[:, t, :], AX.X))
            v.tensor_tensor(before[:, :], tiles_of, earlier[:, :], ALU.mult)
            then(v.tensor_single_scalar(slot_i[:, t], rank_i[:, t], 7, ALU.arith_shift_right))
            v.scalar_tensor_tensor(neg_pos[:, t], slot_i[:, t], float(P), rank_i[:, t], ALU.mult, ALU.subtract)
            v.scalar_tensor_tensor(code[:, t], best[:, t], -float(SLOTS), slot_i[:, t], ALU.mult, ALU.add)
            then(v.reduce_sum(begin[:, :], before[:, :], AX.X))
            place(EARLY, TILES)
            place_positions(EARLY, TILES)
            jobs = count_up[:, 0:JC]
            v.tensor_scalar(pick[:, :], jobs, begin[:, :], tile_of[:, :], ALU.subtract, ALU.is_equal).then_inc(pick_done, 1)
            then(v.tensor_tensor_scan(ends[:, :], tiles_of, tiles_of, 0.0, ALU.add, ALU.bypass))
            then(v.tensor_tensor(past[:, :, :], jobs.unsqueeze(2).to_broadcast([P, JC, E]),
                                 ends[:, :].unsqueeze(1).to_broadcast([P, JC, E]), ALU.is_ge))
            dve.wait_ge(slots_done, 1)
            v.tensor_scalar(from_row[:, :], bank[2][:, 0:JC], -1.0, 0.0, ALU.add, ALU.max).then_inc(from_done, 1)
            then(v.reduce_sum(job[:, :], past[:, :, :], AX.X))
            for turn in range(TURNS + 2):
                j0 = 0 if turn == 0 else FIRST - 2 + (turn - 1) * NG
                last = v.tensor_single_scalar(job_i[:, turn * JW:turn * JW + NG + 3], job[:, j0:j0 + NG + 3], float(E - 1), ALU.min)
            then(last)
            dve.sem_inc(jobs_done, 1)
            then(v.tensor_scalar(empty[:, :], bank[2][:, 0:JC], 0.0, float(NOWHERE + 1), ALU.is_equal, ALU.mult))
            v.scalar_tensor_tensor(to_row[:, :], empty[:, :], -1.0, bank[2][:, 0:JC], ALU.add, ALU.add).then_inc(to_done, 1)

            def part(j, c0, c1):
                return gathered[:, ds(j, 1), c0:c1].rearrange("p a d -> p (a d)")

            def norm_x(q, n):
                j, k = q * NG + n, n % 2
                dve.wait_ge(got_of(n), gathers_by(q, n) * 16)
                after(dve, xft_done, j - 1)
                v.tensor_scalar(xf[:, k, :], part(j, 0, D), part(j, MEAN, MEAN + 1), part(j, RSTD, RSTD + 1),
                                ALU.subtract, ALU.mult).then_inc(xf_done, 1)

            def copy_w1(q, n):
                j, k = q * NG + n, n % 2
                after(dve, gelu_done, j - 1)
                v.tensor_copy(w1_now[:, k, :], w1[:, ds(expert[n] * (F + FC), F + FC)]).then_inc(w1_now_done, 1)

            def finish(q, n):
                j, k, r = q * NG + n, n % 2, n % NG
                dve.wait_ge(y_done, j + 1)
                v.tensor_tensor(yb[:, k, :], bank[4 + k][:, 0:D], b2[:, ds(expert[n] * D, D)], ALU.add).then_inc(yb_done, 1)
                dve.wait_ge(yb_done, j + 1)
                if n >= NG:
                    dve.wait_ge(put[r], (q + n // NG) * 16)
                v.scalar_tensor_tensor(res[:, r, :], yb[:, k, :], part(j, TOP, RW), part(j, 0, D),
                                       ALU.mult, ALU.add).then_inc(res_done, 1)

            expert = {}

            def load_experts(q, n):
                expert.update(experts_of(mybir.EngineType.DVE, q, n))

            def do_job(q, n):
                if has_job(q, n + 1):
                    copy_w1(q, n + 1)
                if has_job(q, n - 2):
                    finish(q, n - 2)
                if has_job(q, n + 2):
                    norm_x(q, n + 2)

            dve.wait_ge(ffn_in, 3 * 16)
            load_experts(0, 0)
            copy_w1(0, 0)
            for n in range(2):
                norm_x(0, n)
            all_jobs(dve, do_job, load_experts)
            finish(0, JOBS - 2)
            finish(0, JOBS - 1)

        @block.gpsimd
        def _(pool):
            g_ = nc.gpsimd
            n_filled = [0]

            def alone(ins):
                n_filled[0] += 1
                ins.then_inc(filled, 1)
                pool.wait_ge(filled, n_filled[0])

            g_.memset(still[:, :], 0.0).then_inc(still_set, 1)
            g_.memset(zero[:, :], 0.0).then_inc(zero_set, 1)
            alone(g_.memset(one[:, :], 1.0))
            alone(g_.memset(neg_half[:, :], -0.5))
            alone(g_.memset(eps[:, :], EPS))
            def prepare_v(h):
                r = slice(h * S, (h + 1) * S)
                alone(g_.memset(v_diag[r, :, :, :, (1 - h) * DK:(2 - h) * DK].rearrange("p b c m d -> p (b c m) d"), 0.0))
                alone(g_.memset(v_diag[r, :, :, :, 2 * DK:VC], 0.0))
                alone(g_.memset(v_diag[r, :, :, :, 2 * DK + h:2 * DK + h + 1], 1.0))

            def invert(g):
                t = slice(g * GT, (g + 1) * GT)
                pool.wait_ge(moments_done, (g + 1) * GT)
                g_.tensor_tensor(rstd1[:, t], moments[:, t, 1], eps[:, t], ALU.add).then_inc(rstd1_in, 1)
                pool.wait_ge(rstd1_in, g + 1)
                g_.tensor_tensor(rstd1[:, t], rstd1[:, t], neg_half[:, t], ALU.pow).then_inc(rstd1_done, 1)

            def zero_k(hp):
                g_.memset(k_diag[:, hp, 2 * GC:GROUPS * GC], 0.0).then_inc(zeroed[2], 1)

            prepare_v(0)
            invert(0)
            pool.wait_ge(rstd1_done, 1)
            prepare_v(1)
            alone(g_.memset(ones[:, :], 1.0))
            pool.sem_inc(v_fixed, 1)
            zero_k(0)
            invert(1)
            pool.wait_ge(const_in, 16)
            pool.wait_ge(q_out, 1)

            def spread_q(b, j):
                after(pool, s_done, b - 1)
                pool.sem_inc(pool_met, 1)
                g_.tensor_tensor(q_par[:, j, :, :], q_t[:, ds(b * S, S)].unsqueeze(1).to_broadcast([P, 2, S]),
                                 parity[:, :].unsqueeze(2).to_broadcast([P, 2, S]), ALU.mult).then_inc(q_par_done, 1)

            def iteration(p):
                if valid(2 * p + 1, B):
                    spread_q(2 * p + 1, 1)
                if at(p, 1) or at(p, 2) or at(p, 3):
                    zero_k(2 * p)
                if at(p, 1):
                    pool.wait_ge(v_out, 8)
                if at(p, GT + 1):
                    pool.wait_ge(v_out, 8 * GROUPS)
                    pool.wait_ge(q_out, GROUPS)
                if valid(2 * p - 1, B):
                    after(pool, pv_done, 2 * p - 2)
                    pool.sem_inc(pool_met, 1)
                    g_.tensor_copy(v_now[:, :, :, :], v_diag[:, ds(2 * p - 1, 1), :, :, :].rearrange("p a c m w -> p (a c) m w")).then_inc(v_now_done, 1)
                if at(p, GT - 1):
                    pool.wait_ge(q_out, 2)
                if valid(2 * p + 2, B):
                    spread_q(2 * p + 2, 0)
                if at(p, 0) or at(p, 1):
                    invert(p + 2)
                if at(p, 0) or at(p, 1) or at(p, 2) or at(p, 3):
                    zero_k(2 * p + 1)
                if valid(p - LAG_XM, TILES):
                    t = p - LAG_XM
                    pool.wait_ge(moments2_done, t + 1)
                    g_.tensor_tensor(vare[:, :], row[:, VAR:RSTD], eps[:, 0:1], ALU.add).then_inc(vare_done, 1)
                    pool.wait_ge(vare_done, t + 1)
                    g_.tensor_tensor(row[:, RSTD:TOP], vare[:, :], neg_half[:, 0:1], ALU.pow).then_inc(rstd2_done, 1)
                    pool.wait_ge(rstd2_done, t + 1)
                    pool.sem_inc(pool_met, 1)
                    g_.tensor_scalar(nshift[:, :], row[:, MEAN:VAR], row[:, RSTD:TOP], -1.0, ALU.mult, ALU.mult).then_inc(nshift_done, 1)

            spread_q(0, 0)
            pipeline(pool, iteration, PEEL, TILES - 2, TILES + LAG_XM)

            pool.wait_ge(rows_out, TILES * 16)

            def gather(j):
                if j >= OWN + NG:
                    pool.wait_ge(xf_done, j - NG + 1)
                pool.sem_inc(pool_met, 1)
                g_.indirect_dma_start(out=gathered[:, j, :], out_offset=None, in_=x_mid,
                                      in_offset=bass.IndirectOffsetOnAxis(ap=from_row[:, j:j + 1].bitcast(u32), axis=0)).then_inc(got_of(j), 16)

            def scatter(j):
                pool.wait_ge(res_done, j + 1)
                pool.sem_inc(pool_met, 1)
                g_.indirect_dma_start(out=a["out"], out_offset=bass.IndirectOffsetOnAxis(ap=to_row[:, j:j + 1].bitcast(u32), axis=0),
                                      in_=res[:, j % NG, :], in_offset=None, bounds_check=TOK - 1, oob_is_err=False).then_inc(put[j % NG], 16)

            pool.wait_ge(from_done, 1)
            for j in range(OWN + NG):
                gather(j)
            pool.wait_ge(to_done, 1)
            for j in range(JOBS):
                scatter(j)
                if OWN + NG + j < JOBS:
                    gather(OWN + NG + j)
            for r in range(NG):
                pool.wait_ge(put[r], len(range(r, JOBS, NG)) * 16)

    return nc


_INS = ["x", "kv_in", "consts", "consts16", "w1", "w2", "b2"]


def kernel(x, ctx_768, L0_xattn_Wq, L0_xattn_Wk, L0_xattn_Wv, L0_xattn_Wo,
           L0_ffn_Wr, L0_ffn_W1, L0_ffn_b1, L0_ffn_W2, L0_ffn_b2):
    import concourse.bacc as bacc
    from concourse.bass_utils import run_bass_kernel_spmd

    c = np.ascontiguousarray
    data = {
        "x": c(np.asarray(x).reshape(TILES, P, D).transpose(1, 0, 2)).reshape(P, TILES * D),
        "ctx_t": c(np.asarray(ctx_768).reshape(TOK, KV).T),
        "wq": c(np.asarray(L0_xattn_Wq).T), "wk": c(np.asarray(L0_xattn_Wk).T),
        "wv": c(np.asarray(L0_xattn_Wv).T),
        "wo": c(np.asarray(L0_xattn_Wo).T.reshape(C, 2, 2, DK, D).transpose(0, 2, 1, 3, 4)).reshape(D, D),
        "wr": c(np.asarray(L0_ffn_Wr)),
        "w1": c(np.concatenate([np.asarray(L0_ffn_W1).transpose(1, 0, 2),
                                np.asarray(L0_ffn_b1).reshape(E, FC, P).transpose(2, 0, 1)], axis=2)).reshape(D, E * (F + FC)),
        "w2": c(np.asarray(L0_ffn_W2).reshape(E, FC, P, D).transpose(2, 0, 1, 3)).reshape(P, E * FC * D),
        "b2": c(np.asarray(L0_ffn_b2)).reshape(E * D),
        "ident": np.eye(P, dtype=np.float32),
        "parity": c(((np.arange(P)[:, None] // DK) % 2 == np.arange(2)[None, :]).astype(np.float32)),
        "own_pair": c(((np.arange(P)[:, None] // (2 * DK)) % 2 == np.arange(2)[None, :]).astype(np.float32)),
        "tri": np.triu(np.ones((P, P), np.float16), 1),
        "first": np.broadcast_to((E - np.arange(E)).astype(np.float32), (P, E)).copy(),
        "token1": (np.arange(P)[:, None] + P * np.arange(TILES)[None, :] + 1).astype(np.float32),
        "position": np.broadcast_to(np.arange(P, dtype=np.float16), (P, P)).copy(),
        "code_row": np.broadcast_to((np.arange(CODES) - CODES).astype(np.float16), (P, CODES)).copy(),
        "earlier": (np.arange(E)[None, :] < np.arange(P)[:, None] // SLOTS).astype(np.float32),
        "tile_of": (np.arange(P) % SLOTS).astype(np.float32).reshape(P, 1),
        "count_up": np.broadcast_to(np.arange(P, dtype=np.float32), (P, P)).copy(),
    }
    for whole, names in (("kv_in", KV_PARTS), ("consts", CONST_PARTS), ("consts16", CONST16_PARTS)):
        data[whole] = np.concatenate([data[n] for n in names], axis=1)
    nc = bacc.Bacc("TRN2", target_bir_lowering=False, num_devices=1)
    arrays, aps = {}, {}
    for name in _INS:
        arrays[f"in_{name}"] = data[name]
        aps[name] = nc.dram_tensor(f"in_{name}", data[name].shape, mybir.dt.from_np(data[name].dtype), kind="ExternalInput").ap()
    aps["out"] = nc.dram_tensor("out_x", [TOK, D], mybir.dt.float32, kind="ExternalOutput").ap()
    build(nc, aps)
    r = run_bass_kernel_spmd(nc, [arrays], core_ids=[0])
    return r.results[0]["out_x"].reshape(B, S, D)
```
